# Optimizing a Trainium2 kernel written in Bass

```python
import numpy as np
import jax
import jax.numpy as jnp

def _softmax(x, axis=-1):
    return jax.nn.softmax(x, axis=axis)

def _gelu(x):
    return jax.nn.gelu(x, approximate=True)

def _silu(x):
    return jax.nn.silu(x)

def _sigmoid(x):
    return jax.nn.sigmoid(x)

def _layernorm(x, axis=-1, eps=1e-05):
    m = jnp.mean(x, axis=axis, keepdims=True)
    v = jnp.var(x, axis=axis, keepdims=True)
    return (x - m) / jnp.sqrt(v + eps)

def _scatter_add(tgt, idx, src, axis=0):
    return tgt.at[idx].add(src)

def _segment_sum(src, seg, n):
    return jax.ops.segment_sum(src, seg, n)
kernel_name = 'mk_flamingo_gated_d2_seqx_r4_4772d9'

def setup_inputs(seed: int=0):
    np.random.seed(seed)
    _w = jnp.asarray

    def _rec_inputs():
        import jax
        import jax.numpy as jnp
        _rk = jax.random.key(seed)
        x = -0.0003929 + 0.9999 * jax.random.normal(jax.random.fold_in(_rk, 1), (2, 1024, 256), jnp.float32)
        _lenS = 1024 - jax.random.randint(jax.random.fold_in(_rk, 7), (2,), 0, max(1, 1024 // 4) + 1, jnp.int32)
        _lenS2 = 64 - jax.random.randint(jax.random.fold_in(_rk, 8), (2,), 0, max(1, 64 // 4) + 1, jnp.int32)
        _ctx_1024P = jax.random.normal(jax.random.fold_in(_rk, 11), (2, 16, 256), jnp.float32)
        _ctx_1024c = jax.random.dirichlet(jax.random.fold_in(_rk, 511), 0.3 * jnp.ones((16,), jnp.float32), (2, 64))
        _ctx_1024t = jnp.einsum('bsk,bkd->bsd', _ctx_1024c, _ctx_1024P)
        _ctx_1024t = _ctx_1024t * jax.lax.rsqrt(jnp.mean(jnp.square(_ctx_1024t)) + 1e-12) * 0.953939
        ctx_1024 = 2.81802e-05 + 1.00001 * (_ctx_1024t + 0.3 * jax.random.normal(jax.random.fold_in(_rk, 611), (2, 64, 256), jnp.float32))
        _g = jax.random.normal(jax.random.fold_in(_rk, 9001), (2, 2), jnp.float32)
        _g = jnp.sign(_g) * jnp.maximum(jnp.abs(_g), 1.0) + (_g == 0) * 1.0
        g_xattn = _g[0]
        g_ffn = _g[1]
        return (x, ctx_1024, g_xattn, g_ffn)
    x, ctx_1024, g_xattn, g_ffn = _rec_inputs()

    def _L0_xattn_setup():
        import jax, jax.numpy as jnp
        import numpy as np
        B, S, C = (8, 512, 256)
        key = jax.random.key(seed)
        ks = jax.random.split(key, 9)
        scale = 1.0 / np.sqrt(C)
        return {'x1': jax.random.normal(ks[0], (B, S, C), jnp.float32), 'x2': jax.random.normal(ks[1], (B, S, C), jnp.float32), 'x3': jax.random.normal(ks[2], (B, S, C), jnp.float32), 'Wq': jax.random.normal(ks[3], (C, C), jnp.float32) * scale, 'bq': jax.random.normal(ks[4], (C,), jnp.float32) * scale, 'Wk': jax.random.normal(ks[5], (C, C), jnp.float32) * scale, 'bk': jax.random.normal(ks[6], (C,), jnp.float32) * scale, 'Wv': jax.random.normal(ks[7], (C, C), jnp.float32) * scale, 'bv': jax.random.normal(ks[8], (C,), jnp.float32) * scale}
    _L0_xattn_all = _L0_xattn_setup()
    _L0_xattn_in = {k: v for k, v in _L0_xattn_all.items() if k in ('Wq', 'bq', 'Wk', 'bk', 'Wv', 'bv')}
    del _L0_xattn_all

    def _L0_ffn_setup():
        import jax, jax.numpy as jnp
        import numpy as np
        B, S, D = (2, 1024, 256)
        H = 128
        E = 16
        K = 2
        key = jax.random.key(seed)
        k1, k2, k3, k4, k5 = jax.random.split(key, 5)
        scale = 0.02
        return {'hidden_states': jax.random.normal(k1, (B, S, D), jnp.float32), 'gate_w': jax.random.normal(k2, (D, E), jnp.float32) * scale, 'w1': jax.random.normal(k3, (E, D, H), jnp.float32) * scale, 'w3': jax.random.normal(k4, (E, D, H), jnp.float32) * scale, 'w2': jax.random.normal(k5, (E, H, D), jnp.float32) * scale}
    _L0_ffn_all = _L0_ffn_setup()
    _L0_ffn_in = {k: v for k, v in _L0_ffn_all.items() if k in ('gate_w', 'w1', 'w3', 'w2')}
    del _L0_ffn_all

    def _L1_xattn_setup():
        import jax, jax.numpy as jnp
        import numpy as np
        D1, D2, D3 = (256, 256, 256)
        key = jax.random.key(seed)
        k1, k2, kw, kb = jax.random.split(key, 4)
        x1 = jax.random.normal(k1, (8, 512, D1), dtype=jnp.float32)
        x2 = jax.random.normal(k2, (8, 512, D2), dtype=jnp.float32)
        bound = 1.0 / np.sqrt(D1 + D2)
        W = jax.random.uniform(kw, (D3, D1 + D2), minval=-bound, maxval=bound, dtype=jnp.float32)
        b = jax.random.uniform(kb, (D3,), minval=-bound, maxval=bound, dtype=jnp.float32)
        return {'x1': x1, 'x2': x2, 'W': W, 'b': b}
    _L1_xattn_all = _L1_xattn_setup()
    _L1_xattn_in = {k: v for k, v in _L1_xattn_all.items() if k in ('W', 'b')}
    del _L1_xattn_all

    def _L1_ffn_setup():
        import jax, jax.numpy as jnp
        import numpy as np
        D_IN, D_HID = (256, 1024)

        def _ternary(key, shape):
            return jax.random.randint(key, shape, -1, 2).astype(jnp.float32)

        def _tlin(x, w, s):
            return jnp.einsum('bsi,oi->bso', x, w) * s
        key = jax.random.key(seed)
        ks = jax.random.split(key, 12)
        inv = lambda fan: 1.0 / np.sqrt(fan).astype(np.float32)
        return {'x': jax.random.normal(ks[0], (4, 512, D_IN), dtype=jnp.float32), 'w1_w': _ternary(ks[1], (D_HID, D_IN)), 'w1_s': jax.random.uniform(ks[2], (D_HID,), dtype=jnp.float32) * inv(D_IN), 'w2_w': _ternary(ks[3], (D_HID, D_IN)), 'w2_s': jax.random.uniform(ks[4], (D_HID,), dtype=jnp.float32) * inv(D_IN), 'h1_w': _ternary(ks[5], (D_HID, D_HID)), 'h1_s': jax.random.uniform(ks[6], (D_HID,), dtype=jnp.float32) * inv(D_HID), 'h2_w': _ternary(ks[7], (D_HID, D_HID)), 'h2_s': jax.random.uniform(ks[8], (D_HID,), dtype=jnp.float32) * inv(D_HID), 'w3_w': _ternary(ks[9], (D_IN, D_HID)), 'w3_s': jax.random.uniform(ks[10], (D_IN,), dtype=jnp.float32) * inv(D_HID)}
    _L1_ffn_all = _L1_ffn_setup()
    _L1_ffn_in = {k: v for k, v in _L1_ffn_all.items() if k in ('w1_w', 'w1_s', 'w2_w', 'w2_s', 'h1_w', 'h1_s', 'h2_w', 'h2_s', 'w3_w', 'w3_s')}
    del _L1_ffn_all
    return {'x': x, 'ctx_1024': ctx_1024, 'g_xattn': g_xattn, 'g_ffn': g_ffn, 'L0_xattn_Wq': _L0_xattn_in['Wq'], 'L0_xattn_bq': _L0_xattn_in['bq'], 'L0_xattn_Wk': _L0_xattn_in['Wk'], 'L0_xattn_bk': _L0_xattn_in['bk'], 'L0_xattn_Wv': _L0_xattn_in['Wv'], 'L0_xattn_bv': _L0_xattn_in['bv'], 'L0_ffn_gate_w': _L0_ffn_in['gate_w'], 'L0_ffn_w1': _L0_ffn_in['w1'], 'L0_ffn_w3': _L0_ffn_in['w3'], 'L0_ffn_w2': _L0_ffn_in['w2'], 'L1_xattn_W': _L1_xattn_in['W'], 'L1_xattn_b': _L1_xattn_in['b'], 'L1_ffn_w1_w': _L1_ffn_in['w1_w'], 'L1_ffn_w1_s': _L1_ffn_in['w1_s'], 'L1_ffn_w2_w': _L1_ffn_in['w2_w'], 'L1_ffn_w2_s': _L1_ffn_in['w2_s'], 'L1_ffn_h1_w': _L1_ffn_in['h1_w'], 'L1_ffn_h1_s': _L1_ffn_in['h1_s'], 'L1_ffn_h2_w': _L1_ffn_in['h2_w'], 'L1_ffn_h2_s': _L1_ffn_in['h2_s'], 'L1_ffn_w3_w': _L1_ffn_in['w3_w'], 'L1_ffn_w3_s': _L1_ffn_in['w3_s']}

def reference(x, ctx_1024, g_xattn, g_ffn, L0_xattn_Wq, L0_xattn_bq, L0_xattn_Wk, L0_xattn_bk, L0_xattn_Wv, L0_xattn_bv, L0_ffn_gate_w, L0_ffn_w1, L0_ffn_w3, L0_ffn_w2, L1_xattn_W, L1_xattn_b, L1_ffn_w1_w, L1_ffn_w1_s, L1_ffn_w2_w, L1_ffn_w2_s, L1_ffn_h1_w, L1_ffn_h1_s, L1_ffn_h2_w, L1_ffn_h2_s, L1_ffn_w3_w, L1_ffn_w3_s):
    import jax
    import jax.numpy as jnp

    def _L0_xattn_ref(x1, x2, x3, Wq, bq, Wk, bk, Wv, bv):
        import jax, jax.numpy as jnp
        import numpy as np
        B, S, C = (8, 512, 256)
        q = jnp.einsum('bsc,dc->bsd', x1, Wq) + bq
        k = jnp.einsum('bsc,dc->bsd', x2, Wk) + bk
        v = jnp.einsum('bsc,dc->bsd', x3, Wv) + bv
        scores = jnp.einsum('bqd,bkd->bqk', q, k)
        attn = jax.nn.softmax(scores, axis=-1)
        return jnp.einsum('bqk,bkd->bqd', attn, v)

    def _L0_ffn_ref(hidden_states, gate_w, w1, w3, w2):
        import jax, jax.numpy as jnp
        import numpy as np
        B, S, D = (2, 1024, 256)
        H = 128
        E = 16
        K = 2
        b, s, d = hidden_states.shape
        x = hidden_states.reshape(-1, d)
        T = x.shape[0]
        scores = jax.nn.softmax(x @ gate_w, axis=-1)
        topk_w, topk_idx = jax.lax.top_k(scores, K)
        topk_w = topk_w / jnp.sum(topk_w, axis=-1, keepdims=True)
        comb = jnp.zeros((T, E), x.dtype).at[jnp.arange(T)[:, None], topk_idx].add(topk_w)
        h = jax.nn.silu(jnp.einsum('td,edh->teh', x, w1)) * jnp.einsum('td,edh->teh', x, w3)
        y = jnp.einsum('teh,ehd,te->td', h, w2, comb)
        return y.reshape(b, s, d) + hidden_states

    def _L1_xattn_ref(x1, x2, W, b):
        import jax, jax.numpy as jnp
        import numpy as np
        D1, D2, D3 = (256, 256, 256)
        d1 = x1.shape[-1]
        W1 = W[:, :d1]
        W2 = W[:, d1:]
        part1 = jnp.einsum('bld,ed->ble', x1, W1)
        part2 = jnp.einsum('bld,ed->be', x2, W2) / x2.shape[1]
        return part1 + part2[:, None, :] + b

    def _L1_ffn_ref(x, w1_w, w1_s, w2_w, w2_s, h1_w, h1_s, h2_w, h2_s, w3_w, w3_s):
        import jax, jax.numpy as jnp
        import numpy as np
        D_IN, D_HID = (256, 1024)

        def _ternary(key, shape):
            return jax.random.randint(key, shape, -1, 2).astype(jnp.float32)

        def _tlin(x, w, s):
            return jnp.einsum('bsi,oi->bso', x, w) * s
        h = jax.nn.silu(_tlin(x, w1_w, w1_s)) * _tlin(x, w2_w, w2_s)
        h = jax.nn.gelu(_tlin(h, h1_w, h1_s), approximate=False)
        h = jax.nn.gelu(_tlin(h, h2_w, h2_s), approximate=False)
        return _tlin(h, w3_w, w3_s)
    x = x + jnp.tanh(g_xattn[0]) * _L0_xattn_ref(_layernorm(x, axis=-1), ctx_1024, ctx_1024, L0_xattn_Wq, L0_xattn_bq, L0_xattn_Wk, L0_xattn_bk, L0_xattn_Wv, L0_xattn_bv)
    x = x + jnp.tanh(g_ffn[0]) * _L0_ffn_ref(_layernorm(x, axis=-1), L0_ffn_gate_w, L0_ffn_w1, L0_ffn_w3, L0_ffn_w2)
    x = x + jnp.tanh(g_xattn[1]) * _L1_xattn_ref(_layernorm(x, axis=-1), ctx_1024, L1_xattn_W, L1_xattn_b)
    x = x + jnp.tanh(g_ffn[1]) * _L1_ffn_ref(_layernorm(x, axis=-1), L1_ffn_w1_w, L1_ffn_w1_s, L1_ffn_w2_w, L1_ffn_w2_s, L1_ffn_h1_w, L1_ffn_h1_s, L1_ffn_h2_w, L1_ffn_h2_s, L1_ffn_w3_w, L1_ffn_w3_s)
    return x

_drawn_inputs = setup_inputs


def setup_inputs(seed=0):
    import zlib

    import numpy as np

    out = dict(_drawn_inputs(seed))
    spreads = {'g_ffn': (-1.0, 0.2)}
    factors = {}
    for name, (base, spread) in spreads.items():
        noise = np.random.default_rng([zlib.crc32(name.encode()), seed]).standard_normal(out[name].shape)
        drawn = base * np.exp(spread * noise) if base else spread * noise
        out[name] = jnp.asarray(drawn.astype(out[name].dtype))
    for name, factor in factors.items():
        out[name] = (out[name] * factor).astype(out[name].dtype)
    return out
```

```python
from contextlib import ExitStack

import concourse.bass as bass
from concourse import mybir

F32 = mybir.dt.float32
F32R = mybir.dt.float32r
I32 = mybir.dt.int32
U32 = mybir.dt.uint32
F16 = mybir.dt.float16
ALU = mybir.AluOpType
ACT = mybir.ActivationFunctionType
AX = mybir.AxisListType

P = 128
D = 256
DK = D // P
T = 2048
NT = T // P
TG = 4
GN = TG * P
NG = NT // TG
NB = 2
KEYS = 64
E = 16
H = 128
TOPK = 2
F = 1024
FK = F // P
PANEL = 512
NPAN = FK + 2 * 2 * FK + DK * FK * P // PANEL
EXP_COLS = DK * 2 * H + D
EPS = 1e-5
NBLK = T * TOPK // P + E
LATE = 16

C_BQ, C_BK, C_S1, C_S2, C_H1, C_H2, C_N = 0, 2, 4, 12, 20, 28, 36
R_BV, R_B1, R_S3, R_G, R_N = 0, 256, 512, 768, 772
K_TRI, K_R = 0, P
K_B = K_R + P
K_E = K_B + NBLK
K_TOK = K_E + E
K_SEG = K_TOK + NT
K_N = K_SEG + E * NT


class Chain:

    def __init__(self, eng, sem):
        self.eng, self.sem, self.n = eng, sem, 0

    def __call__(self, ins):
        self.n += 1
        ins.then_inc(self.sem, 1)

    def done(self):
        self.eng.wait_ge(self.sem, self.n)

    def restart(self):
        self.done()
        self.eng.sem_clear(self.sem)
        self.n = 0


def flamingo_kernel(nc, x, ctxT, cols, rows, wq, wkT, wvT, gate, experts, w1T, w2T, panels, consts, identity, out):
    with ExitStack() as ctx:
        at = [nc.sbuf_base + (-nc.sbuf_base) % 32]

        def place(name, shape, dt=F32, offset=None):
            size = 4
            for n in shape[1:]:
                size *= n
            if offset is None:
                offset = at[0]
                at[0] += size + -size % 32
            return nc.alloc_sbuf_tensor_at(name, shape, dt, offset=offset), offset + size

        def psum(name):
            return ctx.enter_context(nc.psum_tensor(name, [P, 512], F32))

        def sem(name):
            return ctx.enter_context(nc.semaphore(name))

        Wr, w_end = place("Wr", [P, NPAN * PANEL], F32R)
        w_off = w_end - 4 * NPAN * PANEL
        Ah, _ = place("Ah", [P, 4096], F32R)
        Al, _ = place("Al", [P, 4096], F32R)
        Bh, _ = place("Bh", [P, 4096], F32R)
        bl_off = at[0]
        Bl, b_end = place("Bl", [P, 4096], F32R)
        X, _ = place("X", [P, NT, D])
        xt_off = at[0]
        xTh, _ = place("xTh", [P, DK, GN], F32R)
        xTl, _ = place("xTl", [P, DK, GN], F32R)
        sg_off = at[0]
        sg, _ = place("sg", [P, 3, GN])
        xn_off = at[0]
        xn, _ = place("xn", [P, TG, D])
        y2, _ = place("y2", [P, TG, D])
        stage, _ = place("stage", [P, 2, PANEL])
        wlo_off = at[0]
        Wlo, _ = place("Wlo", [P, 2, PANEL], F32R)
        W1h, _ = place("W1h", [P, DK, D], F32R)
        W1l, _ = place("W1l", [P, DK, D], F32R)
        ident, _ = place("ident", [P, P])
        colv, _ = place("colv", [P, C_N])
        tg, _ = place("tg", [P, 4])
        w3s, _ = place("w3s", [P, D])
        crow, _ = place("crow", [P, NB, D])
        stats, _ = place("stats", [P, TG, 6])
        LN = 4
        mv, _ = place("mv", [P, LN, TG, 2])
        veps, _ = place("veps", [P, LN, TG])
        nmean, _ = place("nmean", [P, LN, TG])
        rstd, _ = place("rstd", [P, LN, TG])
        nmr, _ = place("nmr", [P, LN, TG])
        mhalf, _ = place("mhalf", [P, TG])
        ones, _ = place("ones", [1, P])
        wtop, _ = place("wtop", [P, NT, TOPK])
        slots, _ = place("slots", [P, TOPK, NT], U32)
        perm, _ = place("perm", [P, NBLK], U32)
        eoff, _ = place("eoff", [1, NBLK], I32)
        diff, _ = place("diff", [P, NPAN])
        flagf, _ = place("flagf", [P, 2])
        flag, _ = place("flag", [P, 1], I32)
        assert at[0] <= nc.sbuf_usable_end, (at[0], nc.sbuf_usable_end)

        def over(start, end):
            top = [start]

            def put(name, shape, dt=F32):
                size = 2 if dt == F16 else 4
                for n in shape[1:]:
                    size *= n
                offset = top[0]
                top[0] += size + -size % 32
                assert top[0] <= end, (name, top[0], end)
                return nc.alloc_sbuf_tensor_at(name, shape, dt, offset=offset)

            return put

        e_off = w_end - 4 * LATE * PANEL
        put = over(e_off, b_end)
        EH, EL = put("EH", [P, E * EXP_COLS], F32R), put("EL", [P, E * EXP_COLS], F32R)
        put = over(w_off, e_off)
        r_off = w_off
        Wq, WkT, WvT, W2T = (put(n, [P, DK, D]) for n in ("Wq", "WkT", "WvT", "W2T"))
        route_end = w_off + 4 * 4 * DK * D
        rowv = put("rowv", [1, R_N])
        row_off = route_end
        xa_off = w_off + 4 * (4 * DK * D + R_N)
        xa_off += -xa_off % 32
        xa = put("xa", [P, 2, TG, D])
        ctxTs = put("ctxTs", [P, DK, P])
        gw = put("gw", [P, DK, E])
        kT = put("kT", [P, DK, P])
        QK = put("QK", [P, DK, P])
        qkrow = put("qkrow", [1, NB, TG, KEYS])
        V = put("V", [KEYS, NB, D])
        csum = put("csum", [P, DK * NB])
        xb = put("xb", [P, NG, TG, D])
        NES = 4
        ES = put("ES", [P, NES, EXP_COLS])
        put = over(xt_off, sg_off)
        xaT, xbT = put("xaT", [P, DK, GN]), put("xbT", [P, DK, GN])
        put = over(sg_off, xn_off)
        pr = put("pr", [P, 2, TG, KEYS])
        pT = put("pT", [KEYS, GN])
        mx, den, coef = (put(n, [P, TG]) for n in ("mx", "den", "coef"))
        put = over(xn_off, wlo_off)
        W1s = put("W1s", [P, DK, D])
        cmean = put("cmean", [P, DK * NB, P])
        ones128 = put("ones128", [P, P])
        put = over(r_off, route_end)
        lt = put("lt", [P, NT, E])
        eq = put("eq", [P, TOPK, E, NT])
        both = put("both", [P, E, NT])
        inc = put("inc", [P, E, NT])
        pos = put("pos", [P, E, NT])
        picked = put("picked", [P, TOPK, E, NT])
        put = over(row_off, xa_off)
        blk_eq = put("blk_eq", [1, NBLK, E])
        put = over(xa_off, xa_off + 8 * TG * D)
        m8 = put("m8", [P, NT, 8])
        ix8 = put("ix8", [P, NT, 8], U32)
        ixf = put("ixf", [P, NT, TOPK])
        mxr, rden, wsum = (put(n, [P, NT]) for n in ("mxr", "rden", "wsum"))
        cnt, cmod, padded, pinc, pbase = (put(n, [P, E]) for n in ("cnt", "cmod", "padded", "pinc", "pbase"))
        posf, prow, pblk = (put(n, [P, TOPK * NT]) for n in ("posf", "prow", "pblk"))
        cnti, prowi = put("cnti", [P, E], U32), put("prowi", [P, TOPK * NT], U32)
        ohb = put("ohb", [P, TOPK, NT, NBLK], F16)
        esum = put("esum", [1, NBLK])
        put = over(xt_off, sg_off)
        ohr = put("ohr", [P, TOPK * NT, P], F16)
        kc = nc.alloc_sbuf_tensor_at("kc", [P, K_N], F32, offset=wlo_off)
        xg = nc.alloc_sbuf_tensor_at("xg", [P, 4, D], F32, offset=xn_off)
        yb = nc.alloc_sbuf_tensor_at("yb", [P, 4, D], F32, offset=xn_off + 4 * TG * D)
        put = over(xt_off, sg_off)
        bxh, bxl = put("bxh", [P, 2, DK, P], F32R), put("bxl", [P, 2, DK, P], F32R)
        bhh, bhl = put("bhh", [P, 2, H], F32R), put("bhl", [P, 2, H], F32R)
        put = over(sg_off, xn_off)
        bsg, bh = put("bsg", [P, 2, H]), put("bh", [P, 2, H])
        outb = nc.alloc_sbuf_tensor_at("outb", [P, TG, D], F32, offset=bl_off)

        hA = [Ah[:, :].rearrange("p (k t) -> p k t", k=FK), Al[:, :].rearrange("p (k t) -> p k t", k=FK)]
        hB = [Bh[:, :].rearrange("p (k t) -> p k t", k=FK), Bl[:, :].rearrange("p (k t) -> p k t", k=FK)]

        bank = [psum(f"bank{i}") for i in range(8)]

        dma_x, dma_w, held = sem("dma_x"), sem("dma_w"), sem("held")
        dma_pan = [sem("dma_pan0"), sem("dma_pan1")]
        dma_exp = [sem(f"dma_exp{b}") for b in range(NES)]
        dma_xb, dma_ys = sem("dma_xb"), [sem(f"dma_ys{b}") for b in range(4)]
        dma_xg = [sem(f"dma_xg{b}") for b in range(4)]
        dma_yg = sem("dma_yg")
        pool_own, dve_own, act_own = sem("pool_own"), sem("dve_own"), sem("act_own")
        pool_const, pool_flag = sem("pool_const"), sem("pool_flag")
        act_eh, pool_el = sem("act_eh"), sem("pool_el")
        pe_setup, act_setup, dve_setup = sem("pe_setup"), sem("act_setup"), sem("dve_setup")
        dve_flag, act_pan, dve_pan = sem("dve_flag"), sem("act_pan"), sem("dve_pan")
        ln_var, ln_rstd, ln_done = ([sem(f"{n}{i}") for i in range(LN)] for n in ("ln_var", "ln_rstd", "ln_done"))
        pe_xaT, act_xaT, pe_s, dve_s, act_p = (sem(n) for n in ("pe_xaT", "act_xaT", "pe_s", "dve_s", "act_p"))
        dve_den, pe_pT, act_pT, pe_o, dve_x1 = (sem(n) for n in ("dve_den", "pe_pT", "act_pT", "pe_o", "dve_x1"))
        pe_xbT, act_xbT, dve_res = sem("pe_xbT"), sem("act_xbT"), sem("dve_res")
        pe_lg, dve_lt, act_lt, dve_both, pe_rank = (sem(n) for n in ("pe_lg", "dve_lt", "act_lt", "dve_both", "pe_rank"))
        dve_oh, pe_perm, dve_perm = sem("dve_oh"), sem("pe_perm"), sem("dve_perm")
        b_tx, b_xh, b_xl, b_gu, b_si, b_h, b_th, b_hh, b_hl, b_y, b_ye = (sem(f"b_{n}") for n in (
            "tx", "xh", "xl", "gu", "si", "h", "th", "hh", "hl", "y", "ye"))
        f_pe, f_act, f_h, f_hh, f_hl = ([sem(f"{k}{s}") for s in range(FK)] for k in
                                        ("f_pe", "f_act", "f_h", "f_hh", "f_hl"))
        f_w3, f_w3r = [sem("f_w3a"), sem("f_w3b")], sem("f_w3r")
        f_out, f_dma = sem("f_out"), sem("f_dma")
        n_x2, n_T, n_h3, n_l3, n_row, n_p1, n_T4, n_h4, n_l4 = (sem(n) for n in (
            "n_x2", "n_T", "n_h3", "n_l3", "n_row", "n_p1", "n_T4", "n_h4", "n_l4"))
        lo_ready, lo_used = sem("lo_ready"), sem("lo_used")

        block = ctx.enter_context(nc.Block())
        x_tiles = x.rearrange("(t p) d -> p t d", p=P)
        out_tiles = out.rearrange("(t p) d -> p t d", p=P)
        xb_dram = nc.dram_tensor("xb_dram", (T, D), F32, kind="Internal").ap()
        ys_dram = nc.dram_tensor("ys_dram", (NBLK * P, D), F32, kind="Internal").ap()
        SETUP_LOADS = 11

        def blocks(eng, turn, last):
            first, count = 4, (NPAN - LATE - 4) // 4
            for i in range(-1, first):
                turn(i, i)
            with eng.Fori(0, count) as j:
                for c in range(first, first + 4):
                    turn(4 * j + c, c)
            for i in range(first + 4 * count, last + 1):
                turn(i, i)

        def panel_place(w):
            if w < NPAN - LATE:
                return Wr[:, w * PANEL:(w + 1) * PANEL]
            return Wlo[:, w % 2, :]

        def hold(eng, i):
            if not isinstance(i, int):
                eng.sem_inc(held, 1)

        def tiles(g):
            return lambda j: X[:, bass.ds(g * TG + j, 1), :].rearrange("p a d -> p (a d)")

        def group(g):
            return X[:, bass.ds(g * TG, TG), :]

        @block.sync
        def _(eng):
            def load_expert(e):
                if e >= NES:
                    eng.wait_ge(pool_el, e - NES + 1)
                eng.dma_start(ES[:, e % NES, :], experts[e]).then_inc(dma_exp[e % NES], 16)

            eng.dma_start(X[:, 0:TG, :], x_tiles[:, 0:TG, :]).then_inc(dma_x, 16)
            for dst, src in ((ctxTs, ctxT), (WkT, wkT), (Wq, wq), (WvT, wvT), (gw, gate), (W2T, w2T), (W1s, w1T)):
                eng.dma_start(dst[:, :, :], src.rearrange("(k p) n -> p k n", p=P)).then_inc(dma_w, 16)
            for dst, src in ((colv, cols), (rowv, rows), (ident, identity), (kc, consts)):
                eng.dma_start(dst[:, :], src).then_inc(dma_w, 16)
            for g in range(1, NG):
                eng.wait_ge(dma_x, 16 * g)
                eng.dma_start(X[:, g * TG:(g + 1) * TG, :], x_tiles[:, g * TG:(g + 1) * TG, :]).then_inc(dma_x, 16)
            for e in range(NES):
                load_expert(e)
            for b in range(2):
                eng.dma_start(stage[:, b, :], panels[b]).then_inc(dma_pan[b], 16)
            for g in range(NG):
                for e in range(NES + 3 * g, NES + 3 * g + 3):
                    load_expert(e)
                eng.wait_ge(ln_done[1], g + 1)
                eng.dma_start(xb_dram.rearrange("(t p) d -> p t d", p=P)[:, g * TG:(g + 1) * TG, :],
                              xb[:, g, :, :]).then_inc(dma_xb, 16)

            def sp_block(i, c):
                whole = isinstance(i, int)
                if not whole or 0 <= i < NPAN - 2:
                    eng.wait_ge(dve_pan, i + 1)
                    eng.dma_start(stage[:, c % 2, :], panels[i + 2]).then_inc(dma_pan[c % 2], 16)
                if not whole or i >= 2:
                    eng.wait_ge(b_ye, i - 1)
                    eng.dma_start(ys_blocks(i - 2), yb[:, (c - 2) % 4, :]).then_inc(dma_ys[(c - 2) % 4], 16)

            def ys_blocks(i):
                return ys_dram.rearrange("(b p) d -> b p d", p=P)[i]

            blocks(eng, sp_block, NBLK + 1)
            for w in range(LATE):
                if w < 2:
                    eng.wait_ge(dve_pan, NPAN - 1 + w)
                else:
                    eng.wait_ge(act_pan, NPAN + w - 1)
                eng.dma_start(stage[:, w % 2, :], panels[NPAN - LATE + w]).then_inc(dma_pan[w % 2], 16)
            eng.wait_ge(pool_flag, 1)
            general = eng.value_load(flag[0:1, 0:1], min_val=0, max_val=1)
            with eng.If(general == 1):
                eng.wait_ge(act_pan, NPAN + LATE)
                with eng.Fori(0, NG) as g:
                    with eng.Fori(0, NPAN // 2) as j:
                        for b in range(2):
                            eng.wait_ge(lo_ready, g * NPAN + 2 * j + (b + 1))
                            eng.dma_start(stage[:, b, :], panels[2 * j + b]).then_inc(dma_pan[b], 16)
            with eng.Else():
                eng.nop()

        @block.gpsimd
        def _(eng):
            own = Chain(eng, pool_own)
            own(eng.memset(ones[:, :], 1.0))
            for s in (*f_act, *f_hl, f_w3r):
                eng.sem_inc(s, 1)
            for s in (f_dma, *dma_ys):
                eng.sem_inc(s, 16)
            own(eng.memset(mhalf[:, :], -0.5))
            own.done()
            eng.memset(flagf[:, :], 0.0).then_inc(pool_const, 1)

            def factors(which, g):
                eng.wait_ge(ln_var[which], g + 1)
                if not (isinstance(g, int) and g == 0):
                    eng.wait_ge(ln_done[which], g)
                eng.tensor_tensor(rstd[:, which, :], veps[:, which, :], mhalf[:, :], ALU.pow).then_inc(ln_rstd[which], 1)
                eng.wait_ge(ln_rstd[which], 2 * g + 1)
                eng.tensor_tensor(nmr[:, which, :], nmean[:, which, :], rstd[:, which, :],
                                  ALU.mult).then_inc(ln_rstd[which], 1)

            done = [0]

            def split_low(n):
                for e in range(done[0], min(E, done[0] + n)):
                    eng.wait_ge(act_eh, e + 1)
                    eng.tensor_tensor(EL[:, e * EXP_COLS:(e + 1) * EXP_COLS], ES[:, e % NES, :],
                                      EH[:, e * EXP_COLS:(e + 1) * EXP_COLS].bitcast(F32),
                                      ALU.subtract).then_inc(pool_el, 1)
                done[0] += n

            factors(0, 0)
            for k in range(NG + 2):
                if k + 1 < NG:
                    factors(0, k + 1)
                split_low(2)
                if 1 <= k <= NG:
                    factors(1, k - 1)
                split_low(1)
            eng.wait_ge(dve_perm, 1)
            eng.wait_ge(dma_xb, 16 * NG)
            for i in range(NBLK):
                if i >= 4:
                    eng.wait_ge(b_tx, i - 3)
                eng.indirect_dma_start(out=xg[:, i % 4, :], out_offset=None, in_=xb_dram,
                                       in_offset=bass.IndirectOffsetOnAxis(ap=perm[:, i:i + 1], axis=0)
                                       ).then_inc(dma_xg[i % 4], 16)

            def gather_rows(g):
                if g > 0:
                    eng.wait_ge(n_T4, g)
                for j in range(TG):
                    for r, dst in enumerate((xn, y2)):
                        eng.indirect_dma_start(out=dst[:, j, :], out_offset=None, in_=ys_dram,
                                               in_offset=bass.IndirectOffsetOnAxis(
                                                   ap=slots[:, r, g * TG + j:g * TG + j + 1], axis=0)
                                               ).then_inc(dma_yg, 16)

            def add_row(g):
                eng.wait_ge(ln_done[2], g + 1)
                b = g // (NG // NB)
                eng.tensor_tensor(group(g), group(g), crow[:, b:b + 1, :].to_broadcast([P, TG, D]),
                                  ALU.add).then_inc(n_row, 1)

            for b in range(4):
                eng.wait_ge(dma_ys[b], 16 * (NBLK // 4) + 16)
            gather_rows(0)
            eng.wait_ge(dve_flag, 1)
            own(eng.partition_all_reduce(flagf[:, 1:2], flagf[:, 0:1], P, bass.bass_isa.ReduceOp.max))
            own.done()
            eng.tensor_copy(flag[:, :], flagf[:, 1:2]).then_inc(pool_flag, 1)
            eng.wait_ge(pool_flag, 1)
            general = eng.value_load(flag[0:1, 0:1], min_val=0, max_val=1)
            factors(2, 0)
            add_row(0)
            factors(3, 0)

            def low_panels(g, first, last):
                with eng.Fori(first // 2, last // 2) as j:
                    for b in range(2):
                        eng.wait_ge(dma_pan[b], (g * (NPAN // 2) + j) * 16 + ((NPAN + LATE) // 2 + 1) * 16)
                        eng.wait_ge(lo_used, g * NPAN + 2 * j + (b + 1))
                        eng.tensor_tensor(Wlo[:, b, :], stage[:, b, :],
                                          Wr[:, bass.ds((2 * j + b) * PANEL, PANEL)].bitcast(F32),
                                          ALU.subtract).then_inc(lo_ready, 1)

            def front(g):
                gather_rows(g)
                factors(2, g)
                add_row(g)

            with eng.If(general == 1):
                eng.wait_ge(act_pan, NPAN + LATE)
                eng.sem_inc(lo_ready, 2)
                eng.sem_inc(lo_used, 2)
                for g in range(NG):
                    low_panels(g, 0, 2 * FK)
                    if g < NG - 1:
                        front(g + 1)
                    low_panels(g, 2 * FK, 4 * FK)
                    if g < NG - 1:
                        factors(3, g + 1)
                    low_panels(g, 4 * FK, NPAN)
            with eng.Else():
                for g in range(1, NG):
                    front(g)
                    factors(3, g)

        def statistics(eng, own, src, which, g):
            for j in range(TG):
                own(eng.bn_stats(stats[:, j, :], src(j)))
            own.done()
            for j in range(TG):
                own(eng.bn_aggr(mv[:, which, j, :], stats[:, j, :]))
            own.done()
            if not (isinstance(g, int) and g == 0):
                eng.wait_ge(ln_rstd[which], 2 * g)
            own(eng.tensor_scalar(nmean[:, which, :], mv[:, which, :, 0], -1.0, None, ALU.mult))
            own.done()
            eng.tensor_scalar(veps[:, which, :], mv[:, which, :, 1], EPS, None, ALU.add).then_inc(ln_var[which], 1)

        def normalise(eng, src, dst, which, g):
            eng.wait_ge(ln_rstd[which], 2 * g + 2)
            hold(eng, g)
            for j in range(TG):
                ins = eng.activation(dst(j), src(j), ACT.Identity, bias=nmr[:, which, j:j + 1],
                                     scale=rstd[:, which, j:j + 1])
                if j < TG - 1:
                    yield ins
            ins.then_inc(ln_done[which], 1)

        @block.vector
        def _(eng):
            own = Chain(eng, dve_own)
            eng.wait_ge(dma_x, 16)
            statistics(eng, own, tiles(0), 0, 0)
            eng.wait_ge(dma_w, 16 * SETUP_LOADS)
            own(eng.reduce_sum(csum[:, :], ctxTs[:, :, :].rearrange("p k (b n) -> p (k b) n", b=NB), AX.X))
            own(eng.memset(ones128[:, :], 1.0))
            own.done()
            eng.tensor_scalar(cmean[:, :, :], csum[:, :].unsqueeze(2).to_broadcast([P, DK * NB, P]), 1.0 / KEYS, None,
                              ALU.mult).then_inc(dve_setup, 1)
            own(eng.tensor_copy(W1h[:, :, :], W1s[:, :, :]))
            own.done()
            own(eng.tensor_tensor(W1l[:, :, :], W1s[:, :, :], W1h[:, :, :].bitcast(F32), ALU.subtract))
            own(eng.memset(diff[:, :], 0.0))
            eng.wait_ge(pe_setup, 2)
            own(eng.tensor_copy(V[:, :, :], bank[1][0:KEYS, :].rearrange("p (b d) -> p b d", b=NB)))
            eng.wait_ge(pe_setup, 4)
            own(eng.tensor_copy(QK[:, :, :], bank[4][:, 0:DK * P].rearrange("p (k n) -> p k n", k=DK)))
            for b in range(NB):
                own(eng.tensor_copy(qkrow[:, b, :, :], bank[5][0:1, b * KEYS:(b + 1) * KEYS].unsqueeze(1)
                                    .to_broadcast([1, TG, KEYS])))
            eng.wait_ge(act_setup, 3)
            own(eng.tensor_scalar(w3s[:, :], bank[2][:, 0:D], tg[:, 3:4], None, ALU.mult))
            own(eng.tensor_scalar(crow[:, :, :], bank[3][:, :].rearrange("p (b d) -> p b d", b=NB), tg[:, 1:2], None,
                                  ALU.mult))
            own.done()
            eng.memset(eoff[:, :], 0).then_inc(dve_setup, 1)

            def scores_shifted(g):
                eng.wait_ge(pe_s, g + 1)
                sc = bank[2][:, 0:TG * KEYS].rearrange("p (t n) -> p t n", t=TG)
                own(eng.reduce_max(mx[:, :], sc, AX.X))
                own.done()
                eng.tensor_tensor(pr[:, g % 2, :, :], sc, mx[:, :].unsqueeze(2).to_broadcast([P, TG, KEYS]),
                                  ALU.subtract).then_inc(dve_s, 1)

            def weights_sum(g):
                eng.wait_ge(act_p, g + 1)
                own(eng.reduce_sum(den[:, :], pr[:, g % 2, :, :], AX.X))
                own.done()
                own(eng.reciprocal(den[:, :], den[:, :]))
                own.done()
                own(eng.tensor_scalar(coef[:, :], den[:, :], tg[:, 0:1], None, ALU.mult))
                own.done()

            def attended(g):
                eng.wait_ge(pe_o, g + 1)
                for j in range(TG):
                    own(eng.scalar_tensor_tensor(tiles(g)(j), bank[4 + j // 2][:, (j % 2) * D:(j % 2 + 1) * D],
                                                 coef[:, j:j + 1], tiles(g)(j), ALU.mult, ALU.add))
                own.done()
                own(eng.memset(mx[:, 0:1], 0.0))
                own.done()

            def residual(g):
                eng.wait_ge(ln_done[1], g + 1)
                own(eng.scalar_tensor_tensor(group(g), xb[:, g, :, :], tg[:, 2:3], group(g), ALU.mult, ALU.add))

            for k in range(NG + 2):
                if 1 <= k <= NG:
                    weights_sum(k - 1)
                if k + 1 < NG:
                    eng.wait_ge(dma_x, 16 * (k + 2))
                    statistics(eng, own, tiles(k + 1), 0, k + 1)
                if k < NG:
                    scores_shifted(k)
                if 1 <= k <= NG:
                    attended(k - 1)
                    statistics(eng, own, tiles(k - 1), 1, k - 1)
                if k >= 2:
                    residual(k - 2)

            lg = bank[6][:, 0:NT * E].rearrange("p (t e) -> p t e", t=NT)
            c_r, c_b = kc[:, K_R:K_R + P], kc[:, K_B:K_B + NBLK]
            c_e, c_tok, c_seg = kc[:, K_E:K_E + E], kc[:, K_TOK:K_TOK + NT], kc[:, K_SEG:K_SEG + E * NT]
            eng.wait_ge(pe_lg, NG)
            own(eng.reduce_max(mxr[:, :], lg, AX.X))
            own.done()
            eng.tensor_tensor(lt[:, :, :], lg, mxr[:, :].unsqueeze(2).to_broadcast([P, NT, E]),
                              ALU.subtract).then_inc(dve_lt, 1)
            eng.wait_ge(act_lt, 1)
            own(eng.reduce_sum(rden[:, :], lt[:, :, :], AX.X))
            own.done()
            own(eng.reciprocal(rden[:, :], rden[:, :]))
            own.done()
            own(eng.tensor_tensor(lt[:, :, :], lt[:, :, :], rden[:, :].unsqueeze(2).to_broadcast([P, NT, E]), ALU.mult))
            own.done()
            for t in range(NT):
                own(eng.max(m8[:, t, :], lt[:, t, :]))
            own.done()
            for t in range(NT):
                own(eng.max_index(ix8[:, t, :], m8[:, t, :], lt[:, t, :]))
            own.done()
            own(eng.tensor_copy(ixf[:, :, :], ix8[:, :, 0:TOPK]))
            own.done()
            for r in range(TOPK):
                own(eng.tensor_tensor(eq[:, r, :, :], c_e.unsqueeze(2).to_broadcast([P, E, NT]),
                                      ixf[:, :, r].unsqueeze(1).to_broadcast([P, E, NT]), ALU.is_equal))
            own.done()
            eng.tensor_tensor(both[:, :, :], eq[:, 0, :, :], eq[:, 1, :, :], ALU.add).then_inc(dve_both, 1)
            own(eng.tensor_tensor(wsum[:, :], m8[:, :, 0], m8[:, :, 1], ALU.add))
            own.done()
            own(eng.reciprocal(wsum[:, :], wsum[:, :]))
            own.done()
            own(eng.tensor_scalar(wsum[:, :], wsum[:, :], tg[:, 2:3], None, ALU.mult))
            own.done()
            own(eng.tensor_tensor(wtop[:, :, :], m8[:, :, 0:TOPK], wsum[:, :].unsqueeze(2).to_broadcast([P, NT, TOPK]),
                                  ALU.mult))
            rank = bank[0][:, 0:E * NT].rearrange("p (e t) -> p e t", e=E)
            tot = bank[1][:, 0:E * NT].rearrange("p (e t) -> p e t", e=E)
            eng.wait_ge(pe_rank, 1)
            own(eng.tensor_tensor_scan(inc[:, :, :].rearrange("p e t -> p (e t)"), c_seg, bank[1][:, 0:E * NT], 0.0,
                                       ALU.mult, ALU.add))
            own.done()
            own(eng.tensor_scalar(cnt[:, :], inc[:, :, NT - 1], float(P - 1), None, ALU.add))
            own.done()
            own(eng.tensor_copy(cnti[:, :], cnt[:, :]))
            own.done()
            own(eng.tensor_scalar(cnti[:, :], cnti[:, :], P - 1, None, ALU.bitwise_and))
            own.done()
            own(eng.tensor_copy(cmod[:, :], cnti[:, :]))
            own.done()
            own(eng.tensor_tensor(padded[:, :], cnt[:, :], cmod[:, :], ALU.subtract))
            own.done()
            own(eng.tensor_tensor_scan(pinc[:, :], kc[:, K_SEG + 1:K_SEG + 2].to_broadcast([P, E]), padded[:, :], 0.0, ALU.mult, ALU.add))
            own(eng.tensor_tensor(pos[:, :, :], rank, inc[:, :, :], ALU.add))
            own.done()
            own(eng.tensor_tensor(pbase[:, :], pinc[:, :], padded[:, :], ALU.subtract))
            own(eng.tensor_tensor(pos[:, :, :], pos[:, :, :], tot, ALU.subtract))
            own.done()
            own(eng.tensor_tensor(pos[:, :, :], pos[:, :, :], pbase[:, :].unsqueeze(2).to_broadcast([P, E, NT]), ALU.add))
            own.done()
            for r in range(TOPK):
                own(eng.tensor_tensor(picked[:, r, :, :], eq[:, r, :, :], pos[:, :, :], ALU.mult))
            own.done()
            for r in range(TOPK):
                own(eng.reduce_sum(posf[:, r * NT:(r + 1) * NT], picked[:, r, :, :].rearrange("p e t -> p t e"), AX.X))
            own.done()
            own(eng.tensor_copy(slots[:, :, :].rearrange("p r t -> p (r t)"), posf[:, :]))
            own.done()
            own(eng.tensor_scalar(prowi[:, :], slots[:, :, :].rearrange("p r t -> p (r t)"), P - 1, None,
                                  ALU.bitwise_and))
            own.done()
            own(eng.tensor_copy(prow[:, :], prowi[:, :]))
            own.done()
            own(eng.tensor_tensor(pblk[:, :], posf[:, :], prow[:, :], ALU.subtract))
            own(eng.tensor_tensor(ohr[:, :, :], c_r.unsqueeze(1).to_broadcast([P, TOPK * NT, P]),
                                  prow[:, :].unsqueeze(2).to_broadcast([P, TOPK * NT, P]), ALU.is_equal))
            own.done()
            for r in range(TOPK):
                own(eng.tensor_tensor(ohb[:, r, :, :], c_b.unsqueeze(1).to_broadcast([P, NT, NBLK]),
                                      pblk[:, r * NT:(r + 1) * NT].unsqueeze(2).to_broadcast([P, NT, NBLK]),
                                      ALU.is_equal))
            own.done()
            for r in range(TOPK):
                ins = eng.tensor_tensor(ohb[:, r, :, :], ohb[:, r, :, :],
                                        c_tok.unsqueeze(2).to_broadcast([P, NT, NBLK]), ALU.mult)
                ins.then_inc(dve_oh, 1)
            own(eng.tensor_tensor(blk_eq[:, :, :], pinc[0:1, :].unsqueeze(1).to_broadcast([1, NBLK, E]),
                                  c_b[0:1, :].unsqueeze(2).to_broadcast([1, NBLK, E]), ALU.is_le))
            own.done()
            own(eng.reduce_sum(esum[:, :], blk_eq[:, :, :], AX.X))
            own.done()
            own(eng.tensor_scalar(esum[:, :], esum[:, :], float(E - 1), float(EXP_COLS), ALU.min, ALU.mult))
            own.done()
            own(eng.tensor_copy(eoff[:, :], esum[:, :]))
            own.done()
            eng.wait_ge(pe_perm, 1)
            eng.tensor_copy(perm[:, :], bank[2][:, 0:NBLK]).then_inc(dve_perm, 1)

            def low_x(i, b):
                eng.wait_ge(b_xh, i + 1)
                eng.tensor_tensor(bxl[:, b, :, :], bank[b][:, 0:DK * P].rearrange("p (k n) -> p k n", k=DK),
                                  bxh[:, b, :, :].bitcast(F32), ALU.subtract).then_inc(b_xl, 1)

            def product(i, b):
                eng.wait_ge(b_si, i + 1)
                eng.tensor_tensor(bh[:, b, :], bank[2 + b][:, H:2 * H], bsg[:, b, :], ALU.mult).then_inc(b_h, 1)

            def low_h(i, b):
                eng.wait_ge(b_hh, i + 1)
                eng.tensor_tensor(bhl[:, b, :], bank[4 + b][:, 0:P], bhh[:, b, :].bitcast(F32),
                                  ALU.subtract).then_inc(b_hl, 1)

            def check_panel(w, b, rounded):
                eng.wait_ge(act_pan, w + 1)
                eng.scalar_tensor_tensor(stage[:, b, :], stage[:, b, :], 1.0, rounded.bitcast(F32), ALU.mult,
                                         ALU.not_equal, accum_out=diff[:, bass.ds(w, 1)]).then_inc(dve_pan, 1)

            def dve_block(i, c):
                whole = isinstance(i, int)
                if not whole or i + 1 < NBLK:
                    low_x(i + 1, (c + 1) % 2)
                if not whole or 0 <= i < NBLK:
                    product(i, c % 2)
                if not whole or 1 <= i <= NBLK:
                    low_h(i - 1, (c - 1) % 2)
                if not whole:
                    check_panel(i, c % 2, Wr[:, bass.ds(i * PANEL, PANEL)])
                elif i in range(NPAN):
                    check_panel(i, c % 2, panel_place(i))

            eng.wait_ge(dve_perm, 1)
            blocks(eng, dve_block, NBLK + 1)
            own(eng.reduce_max(flagf[:, 0:1], diff[:, :], AX.X))
            own.done()
            eng.tensor_scalar(flagf[:, 0:1], flagf[:, 0:1], 1.0, None, ALU.min).then_inc(dve_flag, 1)
            own.restart()

            def x2(g):
                eng.wait_ge(dma_yg, 16 * 2 * TG * g + 16 * 2 * TG)
                for r, src in enumerate((xn, y2)):
                    for j in range(TG):
                        w = wtop[:, bass.ds(g * TG + j, 1), r:r + 1].rearrange("p a b -> p (a b)")
                        own(eng.scalar_tensor_tensor(tiles(g)(j), src[:, j, :], w, tiles(g)(j), ALU.mult, ALU.add))
                    own.done()
                statistics(eng, own, tiles(g), 2, g)

            def low3(g):
                eng.wait_ge(n_h3, g + 1)
                for k in range(DK):
                    ins = eng.tensor_tensor(xTl[:, k, :], bank[6 + k][:, :], xTh[:, k, :].bitcast(F32), ALU.subtract)
                    if k < DK - 1:
                        own(ins)
                ins.then_inc(n_l3, 1)

            def x3(g):
                eng.wait_ge(n_row, g + 1)
                eng.wait_ge(n_p1, g + 1)
                for q in range(2):
                    rows_ = X[:, bass.ds(g * TG + 2 * q, 2), :].rearrange("p a d -> p (a d)")
                    own(eng.scalar_tensor_tensor(rows_, bank[6 + q][:, :], tg[:, 1:2], rows_, ALU.mult, ALU.add))
                own.done()
                statistics(eng, own, tiles(g), 3, g)

            def low4(g):
                eng.wait_ge(n_h4, g + 1)
                for k in range(DK):
                    ins = eng.tensor_tensor(xTl[:, k, :], bank[6 + k][:, :], xTh[:, k, :].bitcast(F32), ALU.subtract)
                    if k < DK - 1:
                        own(ins)
                ins.then_inc(n_l4, 1)

            def ffn(g, more):
                g3 = 3 * g
                for m in range(FK + 1):
                    if m < FK:
                        eng.wait_ge(f_act[m], g3 + 2)
                        eng.scalar_tensor_tensor(sg[:, m % 3, :], bank[2 * (m % 2) + 1][:, :], colv[:, C_S2 + m:C_S2 + m + 1],
                                                 sg[:, m % 3, :], ALU.mult, ALU.mult).then_inc(f_h[m], 1)
                    if m > 0:
                        eng.wait_ge(f_hh[m - 1], g + 1)
                        eng.tensor_tensor(hA[1][:, m - 1, :], sg[:, (m - 1) % 3, :], hA[0][:, m - 1, :].bitcast(F32),
                                          ALU.subtract).then_inc(f_hl[m - 1], 1)
                for layer, h in ((1, hB), (2, hA)):
                    for m in range(FK):
                        if layer == 1 and m == 0:
                            eng.wait_ge(f_dma, 16 * g + 16)
                        r = (8 * layer + m) % 3
                        eng.wait_ge(f_act[m], g3 + (layer + 2))
                        own(eng.tensor_copy(h[0][:, m, :], sg[:, r, :]))
                        own.done()
                        eng.tensor_tensor(h[1][:, m, :], sg[:, r, :], h[0][:, m, :].bitcast(F32),
                                          ALU.subtract).then_inc(f_hl[m], 1)
                        if more and layer == 1 and m == 1:
                            x2(g + 1)
                        if more and layer == 1 and m == 7:
                            low3(g + 1)
                        if more and layer == 2 and m == 2:
                            x3(g + 1)
                for q in range(2):
                    eng.wait_ge(f_w3[q], g + 1)
                    ins = eng.tensor_tensor(outb[:, 2 * q:2 * q + 2, :], bank[4 + q][:, :].rearrange("p (t d) -> p t d", t=2),
                                            w3s[:, :].unsqueeze(1).to_broadcast([P, 2, D]), ALU.mult)
                    if q == 0:
                        own(ins)
                ins.then_inc(f_w3r, 1)
                eng.wait_ge(f_w3r, g + 2)
                own.done()
                eng.tensor_tensor(outb[:, :, :], outb[:, :, :], group(g), ALU.add).then_inc(f_out, 1)
                if more:
                    low4(g + 1)
                own.restart()

            x2(0)
            low3(0)
            x3(0)
            low4(0)
            own.restart()
            with eng.Fori(0, NG - 1) as g:
                ffn(g, True)
            ffn(NG - 1, False)

        @block.scalar
        def _(eng):
            own = Chain(eng, act_own)

            def norm(src, dst, which, g):
                for ins in normalise(eng, src, dst, which, g):
                    own(ins)

            done = [0]

            def split_high(n):
                for e in range(done[0], min(E, done[0] + n)):
                    eng.wait_ge(dma_exp[e % NES], 16 * (e // NES + 1))
                    eng.activation(EH[:, e * EXP_COLS:(e + 1) * EXP_COLS], ES[:, e % NES, :],
                                   ACT.Copy).then_inc(act_eh, 1)
                done[0] += n

            norm(tiles(0), lambda j: xa[:, 0, j, :], 0, 0)
            eng.wait_ge(pe_setup, 1)
            for d in range(DK):
                eng.activation(kT[:, d, :], bank[0][:, d * P:(d + 1) * P], ACT.Identity,
                               bias=colv[:, C_BK + d:C_BK + d + 1]).then_inc(act_setup, 1)
            eng.wait_ge(pe_setup, 2)
            eng.activation(tg[:, :], bank[2][:, D:D + 4], ACT.Tanh).then_inc(act_setup, 1)

            def empty(dst, b, ready, n, done_sem):
                eng.wait_ge(ready, n)
                for k in range(DK):
                    ins = eng.activation(dst[:, k, :], bank[b + k][:, :], ACT.Copy)
                    ins.then_inc(done_sem, 1)

            for k in range(NG + 2):
                if k < NG:
                    empty(xaT, 0, pe_xaT, k + 1, act_xaT)
                if 1 <= k <= NG:
                    eng.wait_ge(pe_pT, k)
                    eng.activation(pT[:, :], bank[3][0:KEYS, :], ACT.Copy).then_inc(act_pT, 1)
                if k + 1 < NG:
                    if k >= 1:
                        eng.wait_ge(pe_xaT, k)
                    norm(tiles(k + 1), lambda j: xa[:, (k + 1) % 2, j, :], 0, k + 1)
                if k < NG:
                    eng.wait_ge(dve_s, k + 1)
                    eng.activation(pr[:, k % 2, :, :], pr[:, k % 2, :, :], ACT.Exp).then_inc(act_p, 1)
                if k >= 2:
                    empty(xbT, 0, pe_xbT, k - 1, act_xbT)
                split_high(3)
                if 1 <= k <= NG:
                    norm(tiles(k - 1), lambda j: xb[:, k - 1, j, :], 1, k - 1)

            eng.wait_ge(dve_lt, 1)
            eng.activation(lt[:, :, :], lt[:, :, :], ACT.Exp).then_inc(act_lt, 1)

            def high_x(i, b):
                eng.wait_ge(b_tx, i + 1)
                eng.activation(bxh[:, b, :, :].rearrange("p k n -> p (k n)"), bank[b][:, 0:DK * P],
                               ACT.Copy).then_inc(b_xh, 1)

            def silu(i, b):
                eng.wait_ge(b_gu, i + 1)
                eng.activation(bsg[:, b, :], bank[2 + b][:, 0:H], ACT.Silu).then_inc(b_si, 1)

            def high_h(i, b):
                eng.wait_ge(b_th, i + 1)
                eng.activation(bhh[:, b, :], bank[4 + b][:, 0:P], ACT.Copy).then_inc(b_hh, 1)

            def rows_out(i, b, c4):
                eng.wait_ge(b_y, i + 1)
                eng.wait_ge(dma_ys[c4 % 4], 16 * (i // 4) + 16 if isinstance(i, int) else 4 * (i - c4) + 16 * (c4 // 4) + 16)
                eng.activation(yb[:, c4 % 4, :], bank[6 + b][:, 0:D], ACT.Copy).then_inc(b_ye, 1)

            def round_panel(w, c):
                eng.wait_ge(dma_pan[c % 2], 16 * (w // 2) + 16 if isinstance(w, int) else 8 * (w - c) + 16 * (c // 2) + 16)
                dst = panel_place(w) if isinstance(w, int) else Wr[:, bass.ds(w * PANEL, PANEL)]
                if isinstance(w, int) and w >= NPAN - LATE + 2:
                    eng.wait_ge(dve_pan, w - 1)
                hold(eng, w)
                eng.activation(dst, stage[:, c % 2, :], ACT.Copy).then_inc(act_pan, 1)

            def act_block(i, c):
                whole = isinstance(i, int)
                if not whole or i + 1 < NBLK:
                    high_x(i + 1, (c + 1) % 2)
                if not whole or 0 <= i < NBLK:
                    silu(i, c % 2)
                if not whole or 1 <= i <= NBLK:
                    high_h(i - 1, (c - 1) % 2)
                if not whole or i in range(NPAN):
                    round_panel(i, c)
                if not whole or 2 <= i <= NBLK + 1:
                    rows_out(i - 2, c % 2, c - 2)

            blocks(eng, act_block, NBLK + 1)
            for w in range(LATE):
                eng.wait_ge(dma_pan[w % 2], 16 * (NPAN // 2 + w // 2 + 1))
                eng.activation(Wr[:, (NPAN - LATE + w) * PANEL:(NPAN - LATE + w + 1) * PANEL], stage[:, w % 2, :],
                               ACT.Copy).then_inc(act_pan, 1)

            def norm3(g):
                norm(tiles(g), lambda j: xn[:, j, :], 2, g)

            def norm4(g):
                norm(tiles(g), lambda j: xn[:, j, :], 3, g)

            def high(g, ready, done_sem):
                eng.wait_ge(ready, g + 1)
                for k in range(DK):
                    ins = eng.activation(xTh[:, k, :], bank[6 + k][:, :], ACT.Copy)
                    if k < DK - 1:
                        own(ins)
                ins.then_inc(done_sem, 1)

            def ffn(g, more):
                g3 = 3 * g
                for m in range(FK + 1):
                    if m < FK:
                        eng.wait_ge(f_pe[m], g3 + 1)
                        if m < 3:
                            eng.wait_ge(f_hl[m + 5], g3 + 1)
                        else:
                            eng.wait_ge(f_hl[m - 3], g3 + 1 + 1)
                        eng.activation(sg[:, m % 3, :], bank[2 * (m % 2)][:, :], ACT.Silu,
                                       scale=colv[:, C_S1 + m:C_S1 + m + 1]).then_inc(f_act[m], 1)
                    if m > 0:
                        eng.wait_ge(f_h[m - 1], g + 1)
                        eng.activation(hA[0][:, m - 1, :], sg[:, (m - 1) % 3, :], ACT.Copy).then_inc(f_hh[m - 1], 1)
                for layer, c in ((1, C_H1), (2, C_H2)):
                    for m in range(FK):
                        eng.wait_ge(f_pe[m], g3 + (layer + 1))
                        if m < 3:
                            eng.wait_ge(f_hl[m + 5], g3 + layer + 1)
                        else:
                            eng.wait_ge(f_hl[m - 3], g3 + (layer + 1) + 1)
                        eng.activation(sg[:, (8 * layer + m) % 3, :], bank[m % 4][:, :], ACT.Gelu,
                                       scale=colv[:, c + m:c + m + 1]).then_inc(f_act[m], 1)
                        if more and layer == 1 and m == 3:
                            norm3(g + 1)
                        if more and layer == 1 and m == 7:
                            high(g + 1, n_T, n_h3)
                        if more and layer == 2 and m == 4:
                            norm4(g + 1)
                if more:
                    high(g + 1, n_T4, n_h4)
                eng.wait_ge(f_out, g + 1)
                eng.dma_start(out_tiles[:, bass.ds(g * TG, TG), :], outb[:, :, :]).then_inc(f_dma, 16)

            norm3(0)
            high(0, n_T, n_h3)
            norm4(0)
            high(0, n_T4, n_h4)
            with eng.Fori(0, NG - 1) as g:
                ffn(g, True)
            ffn(NG - 1, False)
            eng.wait_ge(f_dma, 16 * NG + 16)

        @block.tensor
        def _(eng):
            mm = eng.matmul

            def three(dst, lhs, rhs, first, last):
                mm(dst, lhs[0], rhs[1], start=first, stop=False)
                mm(dst, lhs[1], rhs[0], start=False, stop=False)
                return mm(dst, lhs[0], rhs[0], start=False, stop=last)

            eng.wait_ge(dma_w, 16 * SETUP_LOADS)
            eng.wait_ge(pool_const, 1)
            for d in range(DK):
                for k in range(DK):
                    ins = mm(bank[0][:, d * P:(d + 1) * P], WkT[:, k, d * P:(d + 1) * P], ctxTs[:, k, :],
                             start=k == 0, stop=k == DK - 1)
            ins.then_inc(pe_setup, 1)
            for b in range(NB):
                dst = bank[1][0:KEYS, b * D:(b + 1) * D]
                mm(dst, ones[:, 0:KEYS], rowv[:, R_BV:R_BV + D], start=True, stop=False)
                for k in range(DK):
                    mm(dst, ctxTs[:, k, b * KEYS:(b + 1) * KEYS], WvT[:, k, :], start=False, stop=k == DK - 1)
            mm(bank[2][:, 0:D + 4], ones[:, :], rowv[:, R_S3:R_G + 4], start=True, stop=True).then_inc(pe_setup, 1)
            eng.wait_ge(dve_setup, 1)
            for b in range(NB):
                dst = bank[3][:, b * D:(b + 1) * D]
                mm(dst, ones[:, :], rowv[:, R_B1:R_B1 + D], start=True, stop=False)
                for k in range(DK):
                    ins = mm(dst, cmean[:, k * NB + b, :], W2T[:, k, :], start=False, stop=k == DK - 1)
            ins.then_inc(pe_setup, 1)
            eng.wait_ge(act_setup, 2)
            for c in range(DK):
                for k in range(DK):
                    mm(bank[4][:, c * P:(c + 1) * P], Wq[:, k, c * P:(c + 1) * P], kT[:, k, :], start=k == 0, stop=k == DK - 1)
            for k in range(DK):
                ins = mm(bank[5][0:1, 0:P], colv[:, C_BQ + k:C_BQ + k + 1], kT[:, k, :], start=k == 0, stop=k == DK - 1)
            ins.then_inc(pe_setup, 1)

            def transposes(src, b, sem_done):
                for k in range(DK):
                    for j in range(TG):
                        ins = eng.transpose(bank[b + k][:, j * P:(j + 1) * P], src[:, j, k * P:(k + 1) * P], ident[:, :])
                ins.then_inc(sem_done, 1)

            def scores(g):
                b = g // (NG // NB)
                eng.wait_ge(act_xaT, 2 * g + 2)
                eng.wait_ge(dve_s, g)
                mm(bank[2][:, 0:TG * KEYS], ones[:, :], qkrow[:, b, :, :].rearrange("p t n -> p (t n)"),
                   start=True, stop=False, skip_group_check=True)
                for j in range(TG):
                    for k in range(DK):
                        ins = mm(bank[2][:, j * KEYS:(j + 1) * KEYS], xaT[:, k, j * P:(j + 1) * P],
                                 QK[:, k, b * KEYS:(b + 1) * KEYS], start=False,
                                 stop=k == DK - 1, skip_group_check=True)
                ins.then_inc(pe_s, 1)

            def attend(g):
                b = g // (NG // NB)
                eng.wait_ge(act_pT, g + 1)
                if g > 0:
                    eng.wait_ge(ln_var[1], g)
                for j in range(TG):
                    ins = mm(bank[4 + j // 2][:, (j % 2) * D:(j % 2 + 1) * D], pT[:, j * P:(j + 1) * P], V[:, b, :],
                             start=True, stop=True)
                ins.then_inc(pe_o, 1)

            def logits(g):
                eng.wait_ge(act_xbT, 2 * g + 2)
                for j in range(TG):
                    t = g * TG + j
                    for k in range(DK):
                        ins = mm(bank[6][:, t * E:(t + 1) * E], xbT[:, k, j * P:(j + 1) * P], gw[:, k, :],
                                 start=k == 0, stop=k == DK - 1)
                ins.then_inc(pe_lg, 1)

            eng.wait_ge(dve_setup, 2)
            for k in range(NG + 2):
                if k < NG:
                    eng.wait_ge(ln_done[0], k + 1)
                    if k >= 3:
                        eng.wait_ge(act_xbT, 2 * (k - 2))
                    transposes(xa[:, k % 2, :, :], 0, pe_xaT)
                if 1 <= k <= NG:
                    eng.wait_ge(act_p, k)
                    for j in range(TG):
                        ins = eng.transpose(bank[3][0:KEYS, j * P:(j + 1) * P], pr[:, (k - 1) % 2, j, :], ident[:, :])
                    ins.then_inc(pe_pT, 1)
                if k < NG:
                    scores(k)
                if k >= 2:
                    eng.wait_ge(ln_done[1], k - 1)
                    if k == NG + 1:
                        eng.wait_ge(act_xbT, 2 * (k - 2))
                    transposes(xb[:, k - 2, :, :], 0, pe_xbT)
                if 1 <= k <= NG:
                    attend(k - 1)
                if k >= 2:
                    logits(k - 2)

            eng.wait_ge(dve_both, 1)
            rhs = both[:, :, :].rearrange("p e t -> p (e t)")
            mm(bank[0][:, 0:E * NT], kc[:, K_TRI:K_TRI + P], rhs, start=True, stop=True)
            mm(bank[1][:, 0:E * NT], ones128[:, :], rhs, start=True, stop=True).then_inc(pe_rank, 1)
            eng.wait_ge(dve_oh, TOPK)
            for n in range(TOPK * NT):
                ins = mm(bank[2][:, 0:NBLK], ohr[:, n, :], ohb[:, n // NT, n % NT, :], start=n == 0, stop=n == TOPK * NT - 1)
            ins.then_inc(pe_perm, 1)

            def load_offset(i):
                return eng.value_load(eoff[0:1, bass.ds(i, 1)], min_val=0, max_val=(E - 1) * EXP_COLS)

            def x_columns(i, b, c4):
                eng.wait_ge(dma_xg[c4 % 4], 16 * (i // 4) + 16 if isinstance(i, int) else 4 * (i - c4) + 16 * (c4 // 4) + 16)
                if not isinstance(i, int) or i >= 2:
                    eng.wait_ge(b_xl, i - 1)
                for k in range(DK):
                    ins = eng.transpose(bank[b][:, k * P:(k + 1) * P], xg[:, c4 % 4, k * P:(k + 1) * P], ident[:, :])
                ins.then_inc(b_tx, 1)

            def gate_up(i, b):
                at_ = load_offset(i)
                eng.wait_ge(b_xl, i + 1)
                if not isinstance(i, int) or i >= 2:
                    eng.wait_ge(b_h, i - 1)
                for k in range(DK):
                    w = bass.ds(at_ + k * 2 * H, 2 * H)
                    ins = three(bank[2 + b][:, 0:2 * H], (bxh[:, b, k, :], bxl[:, b, k, :]), (EH[:, w], EL[:, w]),
                                k == 0, k == DK - 1)
                ins.then_inc(b_gu, 1)

            def h_columns(i, b):
                eng.wait_ge(b_h, i + 1)
                if not isinstance(i, int) or i >= 2:
                    eng.wait_ge(b_hl, i - 1)
                eng.transpose(bank[4 + b][:, 0:P], bh[:, b, :], ident[:, :]).then_inc(b_th, 1)

            def down(i, b):
                at_ = load_offset(i)
                eng.wait_ge(b_hl, i + 1)
                if not isinstance(i, int) or i >= 2:
                    eng.wait_ge(b_ye, i - 1)
                w = bass.ds(at_ + 2 * DK * H, D)
                three(bank[6 + b][:, 0:D], (bhh[:, b, :], bhl[:, b, :]), (EH[:, w], EL[:, w]), True, True).then_inc(b_y, 1)

            def pe_block(i, c):
                whole = isinstance(i, int)
                if not whole or i + 1 < NBLK:
                    x_columns(i + 1, (c + 1) % 2, c + 1)
                if not whole or 0 <= i < NBLK:
                    gate_up(i, c % 2)
                if not whole or 1 <= i <= NBLK:
                    h_columns(i - 1, (c - 1) % 2)
                if not whole or 2 <= i <= NBLK + 1:
                    down(i - 2, c % 2)

            eng.wait_ge(dve_perm, 1)
            eng.wait_ge(pool_el, E)
            blocks(eng, pe_block, NBLK + 1)

            def T3(g):
                eng.wait_ge(ln_done[2], g + 1)
                if not (isinstance(g, int) and g == 0):
                    eng.wait_ge(n_l4, g)
                transposes(xn, 6, n_T)

            def part1(g):
                eng.wait_ge(n_l3, g + 1)
                for j in range(TG):
                    dst = bank[6 + j // 2][:, (j % 2) * D:(j % 2 + 1) * D]
                    for k in range(DK):
                        ins = three(dst, (xTh[:, k, j * P:(j + 1) * P], xTl[:, k, j * P:(j + 1) * P]),
                                    (W1h[:, k, :], W1l[:, k, :]), k == 0, k == DK - 1)
                ins.then_inc(n_p1, 1)

            def T4(g):
                eng.wait_ge(ln_done[3], g + 1)
                transposes(xn, 6, n_T4)

            def ffn(g, more, general):
                g3 = 3 * g
                panel = [0]

                def low_part(count):
                    w = panel[0]
                    panel[0] += 1
                    eng.wait_ge(lo_ready, g * NPAN + (w + 3))
                    return Wlo[:, w % 2, :]

                for m in range(FK):
                    if m >= 2:
                        eng.wait_ge(f_h[m - 2], g + 1)
                    elif m == 0:
                        eng.wait_ge(n_l4, g + 1)
                        eng.wait_ge(f_act[5], g3 + 1)
                    else:
                        eng.wait_ge(f_act[7], g3 + 1)
                    w = Wr[:, m * PANEL:(m + 1) * PANEL].rearrange("p (u k n) -> p u k n", u=2, k=DK)
                    lo = low_part(1).rearrange("p (u k n) -> p u k n", u=2, k=DK) if general else None
                    for u in range(2):
                        dst = bank[2 * (m % 2) + u][:, :]
                        for k in range(DK):
                            mm(dst, w[:, u, k, :], xTh[:, k, :], start=k == 0, stop=False)
                            ins = mm(dst, w[:, u, k, :], xTl[:, k, :], start=False, stop=k == DK - 1 and not general)
                            if general:
                                ins = mm(dst, lo[:, u, k, :], xTh[:, k, :], start=False, stop=k == DK - 1)
                        if general and u == 0:
                            pass
                    ins.then_inc(f_pe[m], 1)
                    if general:
                        eng.wait_ge(f_pe[m], g3 + 1)
                        eng.sem_inc(lo_used, 1)
                for layer, h in ((1, hA), (2, hB)):
                    for m in range(FK):
                        if m < 4:
                            if layer == 1:
                                eng.wait_ge(f_h[6 + m // 2], g + 1)
                            else:
                                eng.wait_ge(f_act[m + 4], g3 + 2 + 1)
                        else:
                            eng.wait_ge(f_act[m - 4], g3 + (layer + 1) + 1)
                        for q in range(2):
                            lo = low_part(1).rearrange("p (k n) -> p k n", k=4) if general else None
                            for kk in range(4):
                                k = 4 * q + kk
                                base = ((2 * layer - 1) * FK + 2 * m + q) * PANEL + kk * P
                                if m == 0:
                                    eng.wait_ge(f_hl[k], g3 + layer + 1)
                                mm(bank[m % 4][:, :], Wr[:, base:base + P], h[0][:, k, :], start=k == 0, stop=False)
                                ins = mm(bank[m % 4][:, :], Wr[:, base:base + P], h[1][:, k, :], start=False,
                                         stop=k == FK - 1 and not general)
                                if general:
                                    ins = mm(bank[m % 4][:, :], lo[:, kk, :], h[0][:, k, :], start=False, stop=k == FK - 1)
                            if general and q == 0:
                                ins.then_inc(lo_used, 1)
                        ins.then_inc(f_pe[m], 1)
                        if general:
                            eng.wait_ge(f_pe[m], g3 + (layer + 1))
                            eng.sem_inc(lo_used, 1)
                        if more and layer == 1 and m == 6:
                            T3(g + 1)
                        if more and layer == 2 and m == 1:
                            part1(g + 1)
                        if more and layer == 2 and m == 6:
                            T4(g + 1)
                eng.wait_ge(f_w3r, g + 1)
                base = 5 * FK * PANEL
                if not general:
                    for j in range(TG):
                        for k in range(FK):
                            if j == 0:
                                eng.wait_ge(f_hl[k], g3 + 3 + 1)
                            w = Wr[:, base + k * D:base + (k + 1) * D]
                            dst = bank[4 + j // 2][:, (j % 2) * D:(j % 2 + 1) * D]
                            mm(dst, hA[0][:, k, j * P:(j + 1) * P], w, start=k == 0, stop=False)
                            ins = mm(dst, hA[1][:, k, j * P:(j + 1) * P], w, start=False, stop=k == FK - 1)
                        if j % 2:
                            ins.then_inc(f_w3[j // 2], 1)
                else:
                    for k in range(FK):
                        if k % 2 == 0:
                            lo = low_part(1).rearrange("p (k n) -> p k n", k=2)
                        eng.wait_ge(f_hl[k], g3 + 3 + 1)
                        w = Wr[:, base + k * D:base + (k + 1) * D]
                        for j in range(TG):
                            dst = bank[4 + j // 2][:, (j % 2) * D:(j % 2 + 1) * D]
                            mm(dst, hA[0][:, k, j * P:(j + 1) * P], w, start=k == 0 and j % 2 == 0, stop=False,
                               skip_group_check=True)
                            mm(dst, hA[1][:, k, j * P:(j + 1) * P], w, start=False, stop=False, skip_group_check=True)
                            ins = mm(dst, hA[0][:, k, j * P:(j + 1) * P], lo[:, k % 2, :], start=False, stop=k == FK - 1,
                                     skip_group_check=True)
                            if k == FK - 1 and j % 2:
                                ins.then_inc(f_w3[j // 2], 1)
                        if k % 2 and k < FK - 1:
                            ins.then_inc(lo_used, 1)
                    eng.wait_ge(f_w3[1], g + 1)
                    eng.sem_inc(lo_used, 1)

            T3(0)
            part1(0)
            T4(0)
            eng.wait_ge(act_pan, NPAN + LATE)
            eng.wait_ge(pool_flag, 1)
            general_flag = eng.value_load(flag[0:1, 0:1], min_val=0, max_val=1)
            with eng.If(general_flag == 1):
                with eng.Fori(0, NG - 1) as g:
                    ffn(g, True, True)
                ffn(NG - 1, False, True)
            with eng.Else():
                with eng.Fori(0, NG - 1) as g:
                    ffn(g, True, False)
                ffn(NG - 1, False, False)


def kernel(**inputs):
    import numpy as np
    import concourse.bacc as bacc
    from concourse import mybir as mb
    from concourse.bass_utils import run_bass_kernel_spmd

    v = {k: np.asarray(a) for k, a in inputs.items()}
    con = np.ascontiguousarray

    def vec(a):
        return con(a.reshape(-1, P).T)

    def row(a):
        return a.reshape(1, -1)

    experts = np.concatenate([
        np.stack([v["L0_ffn_w1"].reshape(E, DK, P, H), v["L0_ffn_w3"].reshape(E, DK, P, H)], 3)
        .transpose(0, 2, 1, 3, 4).reshape(E, P, DK * 2 * H), v["L0_ffn_w2"]], 2)

    def kxm(w):
        return w.T.reshape(w.shape[1] // P, P, w.shape[0] // P, P)

    w12 = np.stack([kxm(v["L1_ffn_w1_w"]), kxm(v["L1_ffn_w2_w"])], 0)
    w12 = w12.transpose(3, 2, 0, 1, 4).reshape(FK, P, PANEL)
    hs = [kxm(v[n]).transpose(2, 1, 0, 3).reshape(FK, P, 2, PANEL).transpose(0, 2, 1, 3).reshape(2 * FK, P, PANEL)
          for n in ("L1_ffn_h1_w", "L1_ffn_h2_w")]
    w3 = v["L1_ffn_w3_w"].T.reshape(FK // 2, 2, P, D).transpose(0, 2, 1, 3).reshape(FK // 2, P, PANEL)
    arrays = {
        "x": v["x"].reshape(T, D),
        "ctxT": v["ctx_1024"].reshape(NB * KEYS, D).T,
        "cols": np.concatenate([vec(v[n]) for n in ("L0_xattn_bq", "L0_xattn_bk", "L1_ffn_w1_s", "L1_ffn_w2_s",
                                                    "L1_ffn_h1_s", "L1_ffn_h2_s")], 1),
        "rows": np.concatenate([row(v[n]) for n in ("L0_xattn_bv", "L1_xattn_b", "L1_ffn_w3_s", "g_xattn", "g_ffn")], 1),
        "wq": v["L0_xattn_Wq"],
        "wkT": v["L0_xattn_Wk"].T,
        "wvT": v["L0_xattn_Wv"].T,
        "gate": v["L0_ffn_gate_w"],
        "experts": experts,
        "w1T": v["L1_xattn_W"][:, :D].T,
        "w2T": v["L1_xattn_W"][:, D:].T,
        "panels": np.concatenate([w12, *hs, w3], 0),
    }
    r, seg = np.arange(P), np.arange(E * NT) % NT != 0
    arrays["consts"] = np.concatenate([
        r[:, None] < r[None, :], np.tile(r, (P, 1)), np.tile(np.arange(NBLK) * P, (P, 1)), np.tile(np.arange(E), (P, 1)),
        np.arange(NT)[None, :] * P + r[:, None], np.tile(seg, (P, 1))], 1).astype(np.float32)
    arrays["identity"] = np.eye(P, dtype=np.float32)
    arrays = {k: con(a) for k, a in arrays.items()}
    nc = bacc.Bacc("TRN2", target_bir_lowering=False, num_devices=1)
    args = [nc.dram_tensor(k, a.shape, mb.dt.from_np(a.dtype), kind="ExternalInput").ap() for k, a in arrays.items()]
    out = nc.dram_tensor("out", (T, D), F32, kind="ExternalOutput").ap()
    flamingo_kernel(nc, *args, out)
    got = run_bass_kernel_spmd(nc, [arrays], core_ids=[0])
    return got.results[0]["out"].reshape(v["x"].shape)
```

```python
from contextlib import ExitStack

import concourse.bass as bass
from concourse import mybir

F32 = mybir.dt.float32
F32R = mybir.dt.float32r
I32 = mybir.dt.int32
U32 = mybir.dt.uint32
F16 = mybir.dt.float16
ALU = mybir.AluOpType
ACT = mybir.ActivationFunctionType
AX = mybir.AxisListType

P = 128
D = 256
DK = D // P
T = 2048
NT = T // P
TG = 4
GN = TG * P
NG = NT // TG
NB = 2
KEYS = 64
E = 16
H = 128
TOPK = 2
F = 1024
FK = F // P
PANEL = 512
NPAN = FK + 2 * 2 * FK + DK * FK * P // PANEL
EXP_COLS = DK * 2 * H + D
EPS = 1e-5
NBLK = T * TOPK // P + E
LATE = 16

C_BQ, C_BK, C_S1, C_S2, C_H1, C_H2, C_N = 0, 2, 4, 12, 20, 28, 36
R_BV, R_B1, R_S3, R_G, R_N = 0, 256, 512, 768, 772
K_TRI, K_R = 0, P
K_B = K_R + P
K_E = K_B + NBLK
K_TOK = K_E + E
K_SEG = K_TOK + NT
K_N = K_SEG + E * NT


class Chain:

    def __init__(self, eng, sem):
        self.eng, self.sem, self.n = eng, sem, 0

    def __call__(self, ins):
        self.n += 1
        ins.then_inc(self.sem, 1)

    def done(self):
        self.eng.wait_ge(self.sem, self.n)

    def restart(self):
        self.done()
        self.eng.sem_clear(self.sem)
        self.n = 0


def flamingo_kernel(nc, x, ctxT, cols, rows, wq, wkT, wvT, gate, experts, w1T, w2T, panels, consts, identity, out):
    with ExitStack() as ctx:
        at = [nc.sbuf_base + (-nc.sbuf_base) % 32]

        def place(name, shape, dt=F32, offset=None):
            size = 4
            for n in shape[1:]:
                size *= n
            if offset is None:
                offset = at[0]
                at[0] += size + -size % 32
            return nc.alloc_sbuf_tensor_at(name, shape, dt, offset=offset), offset + size

        def psum(name):
            return ctx.enter_context(nc.psum_tensor(name, [P, 512], F32))

        def sem(name):
            return ctx.enter_context(nc.semaphore(name))

        Wr, w_end = place("Wr", [P, NPAN * PANEL], F32R)
        w_off = w_end - 4 * NPAN * PANEL
        Ah, _ = place("Ah", [P, 4096], F32R)
        Al, _ = place("Al", [P, 4096], F32R)
        Bh, _ = place("Bh", [P, 4096], F32R)
        bl_off = at[0]
        Bl, b_end = place("Bl", [P, 4096], F32R)
        X, _ = place("X", [P, NT, D])
        xt_off = at[0]
        xTh, _ = place("xTh", [P, DK, GN], F32R)
        xTl, _ = place("xTl", [P, DK, GN], F32R)
        sg_off = at[0]
        sg, _ = place("sg", [P, 3, GN])
        xn_off = at[0]
        xn, _ = place("xn", [P, TG, D])
        y2, _ = place("y2", [P, TG, D])
        stage, _ = place("stage", [P, 2, PANEL])
        wlo_off = at[0]
        Wlo, _ = place("Wlo", [P, 2, PANEL], F32R)
        W1h, _ = place("W1h", [P, DK, D], F32R)
        W1l, _ = place("W1l", [P, DK, D], F32R)
        ident, _ = place("ident", [P, P])
        colv, _ = place("colv", [P, C_N])
        tg, _ = place("tg", [P, 4])
        w3s, _ = place("w3s", [P, D])
        crow, _ = place("crow", [P, NB, D])
        stats, _ = place("stats", [P, TG, 6])
        LN = 4
        mv, _ = place("mv", [P, LN, TG, 2])
        veps, _ = place("veps", [P, LN, TG])
        nmean, _ = place("nmean", [P, LN, TG])
        rstd, _ = place("rstd", [P, LN, TG])
        nmr, _ = place("nmr", [P, LN, TG])
        mhalf, _ = place("mhalf", [P, TG])
        ones, _ = place("ones", [1, P])
        unused, _ = place("unused", [1, 1])
        wtop, _ = place("wtop", [P, NT, TOPK])
        slots, _ = place("slots", [P, TOPK, NT], U32)
        perm, _ = place("perm", [P, NBLK], U32)
        eoff, _ = place("eoff", [1, NBLK + 6], I32)
        diff, _ = place("diff", [P, NPAN])
        flagf, _ = place("flagf", [P, 2])
        flag, _ = place("flag", [P, 1], I32)
        assert at[0] <= nc.sbuf_usable_end, (at[0], nc.sbuf_usable_end)

        def over(start, end):
            top = [start]

            def put(name, shape, dt=F32):
                size = 2 if dt == F16 else 4
                for n in shape[1:]:
                    size *= n
                offset = top[0]
                top[0] += size + -size % 32
                assert top[0] <= end, (name, top[0], end)
                return nc.alloc_sbuf_tensor_at(name, shape, dt, offset=offset)

            return put

        e_off = w_end - 4 * LATE * PANEL
        put = over(e_off, b_end)
        EH, EL = put("EH", [P, E * EXP_COLS], F32R), put("EL", [P, E * EXP_COLS], F32R)
        put = over(w_off, e_off)
        r_off = w_off
        Wq, WkT, WvT, W2T = (put(n, [P, DK, D]) for n in ("Wq", "WkT", "WvT", "W2T"))
        route_end = w_off + 4 * 4 * DK * D
        rowv = put("rowv", [1, R_N])
        row_off = route_end
        xa_off = w_off + 4 * (4 * DK * D + R_N)
        xa_off += -xa_off % 32
        xa = put("xa", [P, 2, TG, D])
        ctxTs = put("ctxTs", [P, DK, P])
        gw = put("gw", [P, DK, E])
        kT = put("kT", [P, DK, P])
        QK = put("QK", [P, DK, P])
        qkrow = put("qkrow", [1, NB, TG, KEYS])
        V = put("V", [KEYS, NB, D])
        csum = put("csum", [P, DK * NB])
        xb = put("xb", [P, NG, TG, D])
        NES = 4
        ES = put("ES", [P, NES, EXP_COLS])
        put = over(xt_off, sg_off)
        xaT, xbT = put("xaT", [P, DK, GN]), put("xbT", [P, DK, GN])
        put = over(sg_off, xn_off)
        pr = put("pr", [P, 2, TG, KEYS])
        pT = put("pT", [KEYS, GN])
        mx, den, coef = (put(n, [P, TG]) for n in ("mx", "den", "coef"))
        put = over(xn_off, wlo_off)
        W1s = put("W1s", [P, DK, D])
        cmean = put("cmean", [P, DK * NB, P])
        ones128 = put("ones128", [P, P])
        put = over(r_off, route_end)
        lt = put("lt", [P, NT, E])
        eq = put("eq", [P, TOPK, E, NT])
        both = put("both", [P, E, NT])
        m8 = put("m8", [P, NT, 8])
        ix8 = put("ix8", [P, NT, 8], U32)
        ixf = put("ixf", [P, NT, TOPK])
        mxr, rden, wsum = (put(n, [P, NT]) for n in ("mxr", "rden", "wsum"))
        kr16, kb16 = put("kr16", [P, P], F16), put("kb16", [P, NBLK], F16)
        prow, pblk = put("prow", [P, TOPK * NT], F16), put("pblk", [P, TOPK * NT], F16)
        put = over(row_off, xa_off)
        blk_eq = put("blk_eq", [1, NBLK, E])
        put = over(xa_off, xa_off + 8 * TG * D)
        inc, pos = put("inc", [P, E, NT]), put("pos", [P, E, NT])
        picked = put("picked", [P, TOPK, E, NT])
        cnt, cmod, padded, pinc, pbase = (put(n, [P, E]) for n in ("cnt", "cmod", "padded", "pinc", "pbase"))
        posf = put("posf", [P, TOPK * NT])
        cnti, prowi = put("cnti", [P, E], U32), put("prowi", [P, TOPK * NT], U32)
        ohb = put("ohb", [P, TOPK, NT, NBLK], F16)
        esum = put("esum", [1, NBLK])
        put = over(xt_off, sg_off)
        ohr = put("ohr", [P, TOPK * NT, P], F16)
        kc = nc.alloc_sbuf_tensor_at("kc", [P, K_N], F32, offset=wlo_off)
        STAGES = 4
        xg = nc.alloc_sbuf_tensor_at("xg", [P, 4, D], F32, offset=xn_off)
        yb = nc.alloc_sbuf_tensor_at("yb", [P, 4, D], F32, offset=xn_off + 4 * TG * D)
        put = over(xt_off, sg_off)
        bxh, bxl = put("bxh", [P, 2, DK, P], F32R), put("bxl", [P, 2, DK, P], F32R)
        bhh, bhl = put("bhh", [P, 2, H], F32R), put("bhl", [P, 2, H], F32R)
        put = over(sg_off, xn_off)
        bsg, bh = put("bsg", [P, 2, H]), put("bh", [P, 2, H])
        stage2 = put("stage2", [P, STAGES - 2, PANEL])
        outb = nc.alloc_sbuf_tensor_at("outb", [P, TG, D], F32, offset=bl_off)

        hA = [Ah[:, :].rearrange("p (k t) -> p k t", k=FK), Al[:, :].rearrange("p (k t) -> p k t", k=FK)]
        hB = [Bh[:, :].rearrange("p (k t) -> p k t", k=FK), Bl[:, :].rearrange("p (k t) -> p k t", k=FK)]

        bank = [psum(f"bank{i}") for i in range(8)]

        dma_x, dma_k, dma_w, held = (sem(n) for n in ("dma_x", "dma_k", "dma_w", "held"))
        dma_pan = [sem(f"dma_pan{b}") for b in range(4)]
        dma_exp = [sem(f"dma_exp{b}") for b in range(NES)]
        dma_xb, dma_ys = sem("dma_xb"), [sem(f"dma_ys{b}") for b in range(4)]
        dma_xg = [sem(f"dma_xg{b}") for b in range(4)]
        dma_yg = [sem(f"dma_yg{j}") for j in range(TG)]
        pool_own, dve_own = sem("pool_own"), sem("dve_own")
        pool_const, pool_flag = sem("pool_const"), sem("pool_flag")
        act_eh, pool_el = sem("act_eh"), sem("pool_el")
        pe_setup, act_setup, dve_setup = sem("pe_setup"), sem("act_setup"), sem("dve_setup")
        dve_flag, act_pan, dve_pan = sem("dve_flag"), sem("act_pan"), sem("dve_pan")
        pool_late = sem("pool_late")
        ln_var, ln_rstd, ln_done = ([sem(f"{n}{i}") for i in range(LN)] for n in ("ln_var", "ln_rstd", "ln_done"))
        pe_xaT, act_xaT, pe_s, dve_s, act_p = (sem(n) for n in ("pe_xaT", "act_xaT", "pe_s", "dve_s", "act_p"))
        pe_pT, act_pT, pe_o, pe_xbT, act_xbT = (sem(n) for n in ("pe_pT", "act_pT", "pe_o", "pe_xbT", "act_xbT"))
        pe_lg, dve_lt, act_lt, dve_both, pe_rank = (sem(n) for n in ("pe_lg", "dve_lt", "act_lt", "dve_both", "pe_rank"))
        dve_oh, pe_perm, dve_perm = sem("dve_oh"), sem("pe_perm"), sem("dve_perm")
        b_tx, b_xh, b_xl, b_gu, b_si, b_h, b_th, b_hh, b_hl, b_y, b_ye = (sem(f"b_{n}") for n in (
            "tx", "xh", "xl", "gu", "si", "h", "th", "hh", "hl", "y", "ye"))
        f_pe, f_act, f_h, f_hh, f_hl = ([sem(f"{k}{s}") for s in range(FK)] for k in
                                        ("f_pe", "f_act", "f_h", "f_hh", "f_hl"))
        f_w3, f_w3r = [sem("f_w3a"), sem("f_w3b")], sem("f_w3r")
        f_out, f_dma = sem("f_out"), sem("f_dma")
        n_T, n_h3, n_l3, n_row, n_p1, n_T4, n_h4, n_l4 = (sem(n) for n in (
            "n_T", "n_h3", "n_l3", "n_row", "n_p1", "n_T4", "n_h4", "n_l4"))
        lo_ready, lo_used = sem("lo_ready"), sem("lo_used")

        block = ctx.enter_context(nc.Block())
        x_tiles = x.rearrange("(t p) d -> p t d", p=P)
        out_tiles = out.rearrange("(t p) d -> p t d", p=P)
        xb_dram = nc.dram_tensor("xb_dram", (T, D), F32, kind="Internal").ap()
        ys_dram = nc.dram_tensor("ys_dram", (NBLK * P, D), F32, kind="Internal").ap()
        KEY_LOADS, OTHER_LOADS = 5, 6
        BODY = 8

        def blocks(eng, turn, last, before=None):
            first, count = 4, (NPAN - LATE - 4) // BODY
            for i in range(-1, first):
                if before and i == 0:
                    before(i, i)
                turn(i, i)
            with eng.Fori(0, count) as j:
                if before:
                    before(BODY * j + first, first)
                for c in range(first, first + BODY):
                    turn(BODY * j + c, c)
            for i in range(first + BODY * count, last + 1):
                if before and (i - first) % BODY == 0:
                    before(i, i)
                turn(i, i)

        def panel_stage(c):
            c %= STAGES
            return stage[:, c, :] if c < 2 else stage2[:, c - 2, :]

        def panel_place(w):
            if w < NPAN - LATE:
                return Wr[:, w * PANEL:(w + 1) * PANEL]
            return Wlo[:, w % 2, :]

        def hold(eng, i):
            if not isinstance(i, int):
                eng.sem_inc(held, 1)

        def tiles(g):
            return lambda j: X[:, bass.ds(g * TG + j, 1), :].rearrange("p a d -> p (a d)")

        def group(g):
            return X[:, bass.ds(g * TG, TG), :]

        @block.sync
        def _(eng):
            def load_expert(e):
                if e >= NES:
                    eng.wait_ge(pool_el, e - NES + 1)
                eng.dma_start(ES[:, e % NES, :], experts[e]).then_inc(dma_exp[e % NES], 16)

            eng.dma_start(X[:, 0:TG, :], x_tiles[:, 0:TG, :]).then_inc(dma_x, 16)
            for dst, src in ((ctxTs, ctxT), (WkT, wkT), (Wq, wq)):
                eng.dma_start(dst[:, :, :], src.rearrange("(k p) n -> p k n", p=P)).then_inc(dma_k, 16)
            for dst, src in ((colv, cols), (ident, identity)):
                eng.dma_start(dst[:, :], src).then_inc(dma_k, 16)
            for dst, src in ((WvT, wvT), (gw, gate), (W2T, w2T), (W1s, w1T)):
                eng.dma_start(dst[:, :, :], src.rearrange("(k p) n -> p k n", p=P)).then_inc(dma_w, 16)
            for dst, src in ((rowv, rows), (kc, consts)):
                eng.dma_start(dst[:, :], src).then_inc(dma_w, 16)
            for g in range(1, NG):
                eng.wait_ge(dma_x, 16 * g)
                eng.dma_start(X[:, g * TG:(g + 1) * TG, :], x_tiles[:, g * TG:(g + 1) * TG, :]).then_inc(dma_x, 16)
            for e in range(NES):
                load_expert(e)
            for b in range(2):
                eng.dma_start(stage[:, b, :], panels[b]).then_inc(dma_pan[b], 16)
            for g in range(NG):
                for e in range(NES + 3 * g, NES + 3 * g + 3):
                    load_expert(e)
                eng.wait_ge(ln_done[1], TG * (g + 1))
                eng.dma_start(xb_dram.rearrange("(t p) d -> p t d", p=P)[:, g * TG:(g + 1) * TG, :],
                              xb[:, g, :, :]).then_inc(dma_xb, 16)

            def sp_block(i, c):
                whole = isinstance(i, int)
                if c == -1:
                    eng.wait_ge(dve_perm, 1)
                    for b in range(2, STAGES):
                        eng.dma_start(panel_stage(b), panels[b]).then_inc(dma_pan[b], 16)
                if not whole or 1 <= i <= NPAN - STAGES:
                    eng.wait_ge(dve_pan, i)
                    eng.dma_start(panel_stage(c - 1), panels[i + (STAGES - 1)]).then_inc(dma_pan[(c - 1) % STAGES], 16)
                if not whole or i >= 2:
                    eng.wait_ge(b_ye, i - 1)
                    eng.dma_start(ys_blocks(i - 2), yb[:, (c - 2) % 4, :]).then_inc(dma_ys[(c - 2) % 4], 16)

            def ys_blocks(i):
                return ys_dram.rearrange("(b p) d -> b p d", p=P)[i]

            blocks(eng, sp_block, NBLK + 1)
            for w in range(LATE):
                if w < 2:
                    eng.wait_ge(dve_pan, NPAN - STAGES + 1 + w)
                else:
                    eng.wait_ge(pool_late, w - 1)
                eng.dma_start(stage[:, w % 2, :], panels[NPAN - LATE + w]).then_inc(dma_pan[w % 2], 16)

            def store_result(g):
                if g < NG - 1:
                    eng.wait_ge(f_out, g + 1)
                    eng.dma_start(out_tiles[:, g * TG:(g + 1) * TG, :], outb[:, :, :]).then_inc(f_dma, 16)
                    return
                for q in range(2):
                    eng.wait_ge(f_out, g + q + 1)
                    eng.dma_start(out_tiles[:, g * TG + 2 * q:g * TG + 2 * q + 2, :],
                                  outb[:, 2 * q:2 * q + 2, :]).then_inc(f_dma, 16)

            eng.wait_ge(pool_flag, 1)
            general = eng.value_load(flag[0:1, 0:1], min_val=0, max_val=1)
            with eng.If(general == 1):
                eng.wait_ge(pool_late, LATE)
                for g in range(NG):
                    with eng.Fori(0, NPAN // 2) as j:
                        for b in range(2):
                            eng.wait_ge(lo_ready, 2 * j + (g * NPAN + b + 1))
                            eng.dma_start(stage[:, b, :], panels[2 * j + b]).then_inc(dma_pan[b], 16)
                    store_result(g)
            with eng.Else():
                for g in range(NG):
                    store_result(g)
            eng.wait_ge(f_dma, 16 * (NG + 1) + 16)

        @block.gpsimd
        def _(eng):
            own = Chain(eng, pool_own)
            own(eng.memset(ones[:, :], 1.0))
            for s in (*f_act, *f_hl, f_w3r):
                eng.sem_inc(s, 1)
            for s in (f_dma, *dma_ys):
                eng.sem_inc(s, 16)
            own(eng.memset(mhalf[:, :], -0.5))
            own.done()
            eng.memset(flagf[:, :], 0.0).then_inc(pool_const, 1)

            def factors(which, g):
                eng.wait_ge(ln_var[which], g + 1)
                if not (isinstance(g, int) and g == 0):
                    eng.wait_ge(ln_done[which], TG * g)
                eng.tensor_tensor(rstd[:, which, :], veps[:, which, :], mhalf[:, :], ALU.pow).then_inc(ln_rstd[which], 1)
                eng.wait_ge(ln_rstd[which], 2 * g + 1)
                eng.tensor_tensor(nmr[:, which, :], nmean[:, which, :], rstd[:, which, :],
                                  ALU.mult).then_inc(ln_rstd[which], 1)

            done = [0]

            def split_low(n):
                for e in range(done[0], min(E, done[0] + n)):
                    eng.wait_ge(act_eh, e + 1)
                    eng.tensor_tensor(EL[:, e * EXP_COLS:(e + 1) * EXP_COLS], ES[:, e % NES, :],
                                      EH[:, e * EXP_COLS:(e + 1) * EXP_COLS].bitcast(F32),
                                      ALU.subtract).then_inc(pool_el, 1)
                done[0] += n

            factors(0, 0)
            for k in range(NG + 2):
                if k + 1 < NG:
                    factors(0, k + 1)
                if k < NG:
                    split_low(2)
                if 1 <= k <= NG:
                    factors(1, k - 1)
                split_low(1 if k < NG else 3)
            eng.wait_ge(dve_perm, 1)
            eng.wait_ge(dma_xb, 16 * NG)
            for i in range(NBLK):
                if i >= 4:
                    eng.wait_ge(b_tx, i - 3)
                eng.indirect_dma_start(out=xg[:, i % 4, :], out_offset=None, in_=xb_dram,
                                       in_offset=bass.IndirectOffsetOnAxis(ap=perm[:, i:i + 1], axis=0)
                                       ).then_inc(dma_xg[i % 4], 16)

            def gather_rows(g):
                if g > 0:
                    eng.wait_ge(n_T4, g)
                for j in range(TG):
                    for r, dst in enumerate((xn, y2)):
                        eng.indirect_dma_start(out=dst[:, j, :], out_offset=None, in_=ys_dram,
                                               in_offset=bass.IndirectOffsetOnAxis(
                                                   ap=slots[:, r, g * TG + j:g * TG + j + 1], axis=0)
                                               ).then_inc(dma_yg[j], 16)

            def add_row(g):
                eng.wait_ge(ln_done[2], TG * (g + 1))
                b = g // (NG // NB)
                eng.tensor_tensor(group(g), group(g), crow[:, b:b + 1, :].to_broadcast([P, TG, D]),
                                  ALU.add).then_inc(n_row, 1)

            for b in range(4):
                eng.wait_ge(dma_ys[b], 16 * (NBLK // 4) + 16)
            gather_rows(0)
            eng.wait_ge(dve_flag, 1)
            own(eng.partition_all_reduce(flagf[:, 1:2], flagf[:, 0:1], P, bass.bass_isa.ReduceOp.max))
            own.done()
            eng.tensor_copy(flag[:, :], flagf[:, 1:2]).then_inc(pool_flag, 1)
            eng.wait_ge(pool_flag, 1)
            general = eng.value_load(flag[0:1, 0:1], min_val=0, max_val=1)

            def late_panels(first, last):
                for w in range(first, last):
                    eng.wait_ge(dma_pan[w % 2], 16 * (NPAN // STAGES + w // 2 + 1))
                    eng.tensor_copy(Wr[:, (NPAN - LATE + w) * PANEL:(NPAN - LATE + w + 1) * PANEL],
                                    stage[:, w % 2, :]).then_inc(pool_late, 1)

            late_panels(0, 1)
            factors(2, 0)
            late_panels(1, 2)
            add_row(0)
            late_panels(2, 4)
            factors(3, 0)
            late_panels(4, LATE)

            def low_panels(g, first, last):
                with eng.Fori(first // 2, last // 2) as j:
                    for b in range(2):
                        eng.wait_ge(dma_pan[b], (g * (NPAN // 2) + j) * 16 + (NPAN // STAGES + LATE // 2 + 1) * 16)
                        eng.wait_ge(lo_used, g * NPAN + 2 * j + (b + 1))
                        eng.tensor_tensor(Wlo[:, b, :], stage[:, b, :],
                                          Wr[:, bass.ds((2 * j + b) * PANEL, PANEL)].bitcast(F32),
                                          ALU.subtract).then_inc(lo_ready, 1)

            def add_residual(g):
                eng.wait_ge(f_w3r, 2 * g + 3)
                eng.tensor_tensor(outb[:, :, :], outb[:, :, :], group(g), ALU.add).then_inc(f_out, 1)

            def front(g):
                gather_rows(g)
                factors(2, g)
                add_row(g)

            with eng.If(general == 1):
                eng.wait_ge(act_pan, NPAN)
                eng.wait_ge(pool_late, LATE)
                eng.sem_inc(lo_ready, 2)
                eng.sem_inc(lo_used, 2)
                for g in range(NG):
                    low_panels(g, 0, 2 * FK)
                    if g < NG - 1:
                        front(g + 1)
                    low_panels(g, 2 * FK, 4 * FK)
                    if g < NG - 1:
                        factors(3, g + 1)
                    low_panels(g, 4 * FK, NPAN)
                    if g < NG - 1:
                        add_residual(g)
            with eng.Else():
                for g in range(NG - 1):
                    front(g + 1)
                    factors(3, g + 1)
                    add_residual(g)

        def statistics(eng, own, src, which, g, make=None):
            made = {}

            def make_next(j):
                if make and j < TG:
                    make(j)
                    made[j] = own.n

            make_next(0)
            for j in range(TG):
                make_next(j + 1)
                if make:
                    eng.wait_ge(own.sem, made[j])
                own(eng.bn_stats(stats[:, j, :], src(j)))
            own.done()
            for j in range(TG):
                own(eng.bn_aggr(mv[:, which, j, :], stats[:, j, :]))
            own.done()
            if not (isinstance(g, int) and g == 0):
                eng.wait_ge(ln_rstd[which], 2 * g)
            own(eng.tensor_scalar(nmean[:, which, :], mv[:, which, :, 0], -1.0, None, ALU.mult))
            own.done()
            eng.tensor_scalar(veps[:, which, :], mv[:, which, :, 1], EPS, None, ALU.add).then_inc(ln_var[which], 1)

        def normalise(eng, src, dst, which, g):
            eng.wait_ge(ln_rstd[which], 2 * g + 2)
            hold(eng, g)
            for j in range(TG):
                ins = eng.activation(dst(j), src(j), ACT.Identity, bias=nmr[:, which, j:j + 1],
                                     scale=rstd[:, which, j:j + 1])
                ins.then_inc(ln_done[which], 1)

        @block.vector
        def _(eng):
            own = Chain(eng, dve_own)
            eng.wait_ge(dma_x, 16)
            statistics(eng, own, tiles(0), 0, 0)
            eng.wait_ge(dma_k, 16 * KEY_LOADS)
            own(eng.reduce_sum(csum[:, :], ctxTs[:, :, :].rearrange("p k (b n) -> p (k b) n", b=NB), AX.X))
            own(eng.memset(ones128[:, :], 1.0))
            own.done()
            eng.tensor_scalar(cmean[:, :, :], csum[:, :].unsqueeze(2).to_broadcast([P, DK * NB, P]), 1.0 / KEYS, None,
                              ALU.mult).then_inc(dve_setup, 1)
            eng.wait_ge(pe_setup, 2)
            own(eng.tensor_copy(QK[:, :, :], bank[4][:, 0:DK * P].rearrange("p (k n) -> p k n", k=DK)))
            for b in range(NB):
                own(eng.tensor_copy(qkrow[:, b, :, :], bank[5][0:1, b * KEYS:(b + 1) * KEYS].unsqueeze(1)
                                    .to_broadcast([1, TG, KEYS])))
            own.done()
            eng.memset(eoff[:, :], 0).then_inc(dve_setup, 1)

            def rest_of_setup():
                eng.wait_ge(dma_w, 16 * OTHER_LOADS)
                eng.wait_ge(pe_setup, 4)
                own(eng.tensor_copy(V[:, :, :], bank[7][0:KEYS, :].rearrange("p (b d) -> p b d", b=NB)))
                eng.wait_ge(act_setup, 3)
                own(eng.tensor_scalar(w3s[:, :], bank[6][:, 0:D], tg[:, 3:4], None, ALU.mult))
                own(eng.tensor_scalar(crow[:, :, :], bank[3][:, :].rearrange("p (b d) -> p b d", b=NB), tg[:, 1:2],
                                      None, ALU.mult))
                own.done()
                eng.memset(diff[:, :], 0.0).then_inc(dve_setup, 1)
                own(eng.tensor_copy(W1h[:, :, :], W1s[:, :, :]))
                own.done()
                own(eng.tensor_tensor(W1l[:, :, :], W1s[:, :, :], W1h[:, :, :].bitcast(F32), ALU.subtract))

            def scores_shifted(g):
                eng.wait_ge(pe_s, g + 1)
                sc = bank[2][:, 0:TG * KEYS].rearrange("p (t n) -> p t n", t=TG)
                own(eng.reduce_max(mx[:, :], sc, AX.X))
                own.done()
                eng.tensor_tensor(pr[:, g % 2, :, :], sc, mx[:, :].unsqueeze(2).to_broadcast([P, TG, KEYS]),
                                  ALU.subtract).then_inc(dve_s, 1)

            def weights_sum(g):
                eng.wait_ge(act_p, g + 1)
                own(eng.reduce_sum(den[:, :], pr[:, g % 2, :, :], AX.X))
                own.done()
                own(eng.reciprocal(den[:, :], den[:, :]))
                own.done()
                own(eng.tensor_scalar(coef[:, :], den[:, :], tg[:, 0:1], None, ALU.mult))
                own.done()

            def attended(g):
                def make(j):
                    eng.wait_ge(pe_o, 2 * g + j // 2 + 1)
                    own(eng.scalar_tensor_tensor(tiles(g)(j), bank[4 + j // 2][:, (j % 2) * D:(j % 2 + 1) * D],
                                                 coef[:, j:j + 1], tiles(g)(j), ALU.mult, ALU.add))

                statistics(eng, own, tiles(g), 1, g, make)

            def residual(g):
                eng.wait_ge(ln_done[1], TG * (g + 1))
                own(eng.scalar_tensor_tensor(group(g), xb[:, g, :, :], tg[:, 2:3], group(g), ALU.mult, ALU.add))

            c_r, c_b = kc[:, K_R:K_R + P], kc[:, K_B:K_B + NBLK]
            c_e, c_tok, c_seg = kc[:, K_E:K_E + E], kc[:, K_TOK:K_TOK + NT], kc[:, K_SEG:K_SEG + E * NT]

            def logits_shifted(g):
                eng.wait_ge(pe_lg, g + 1)
                lg = bank[6 + g % 2][:, 0:TG * E].rearrange("p (t e) -> p t e", t=TG)
                ts = slice(g * TG, (g + 1) * TG)
                own(eng.reduce_max(mxr[:, ts], lg, AX.X))
                own.done()
                eng.tensor_tensor(lt[:, ts, :], lg, mxr[:, ts].unsqueeze(2).to_broadcast([P, TG, E]),
                                  ALU.subtract).then_inc(dve_lt, 1)

            def two_largest(g):
                eng.wait_ge(act_lt, g + 1)
                ts = slice(g * TG, (g + 1) * TG)
                own(eng.reduce_sum(rden[:, ts], lt[:, ts, :], AX.X))
                own.done()
                own(eng.reciprocal(rden[:, ts], rden[:, ts]))
                own.done()
                own(eng.tensor_tensor(lt[:, ts, :], lt[:, ts, :], rden[:, ts].unsqueeze(2).to_broadcast([P, TG, E]),
                                      ALU.mult))
                own.done()
                for t in range(g * TG, (g + 1) * TG):
                    own(eng.max(m8[:, t, :], lt[:, t, :]))
                own.done()
                for t in range(g * TG, (g + 1) * TG):
                    own(eng.max_index(ix8[:, t, :], m8[:, t, :], lt[:, t, :]))
                own.done()
                own(eng.tensor_copy(ixf[:, ts, :], ix8[:, ts, 0:TOPK]))
                own.done()
                for r in range(TOPK):
                    own(eng.tensor_tensor(eq[:, r, :, ts], c_e.unsqueeze(2).to_broadcast([P, E, TG]),
                                          ixf[:, ts, r].unsqueeze(1).to_broadcast([P, E, TG]), ALU.is_equal))
                own.done()
                eng.tensor_tensor(both[:, :, ts], eq[:, 0, :, ts], eq[:, 1, :, ts], ALU.add).then_inc(dve_both, 1)

            for k in range(NG + 3):
                if k >= 3:
                    logits_shifted(k - 3)
                if 1 <= k <= NG:
                    weights_sum(k - 1)
                if k + 1 < NG:
                    eng.wait_ge(dma_x, 16 * (k + 2))
                    statistics(eng, own, tiles(k + 1), 0, k + 1)
                if 1 <= k <= NG:
                    attended(k - 1)
                if k < NG:
                    scores_shifted(k)
                if k == 0:
                    rest_of_setup()
                if 2 <= k < NG + 2:
                    residual(k - 2)
                if k == 3:
                    own(eng.tensor_copy(kr16[:, :], c_r))
                    own(eng.tensor_copy(kb16[:, :], c_b))
                if k >= 3:
                    two_largest(k - 3)

            own(eng.tensor_tensor(wsum[:, :], m8[:, :, 0], m8[:, :, 1], ALU.add))
            own.done()
            own(eng.reciprocal(wsum[:, :], wsum[:, :]))
            own.done()
            own(eng.tensor_scalar(wsum[:, :], wsum[:, :], tg[:, 2:3], None, ALU.mult))
            own.done()
            own(eng.tensor_tensor(wtop[:, :, :], m8[:, :, 0:TOPK], wsum[:, :].unsqueeze(2).to_broadcast([P, NT, TOPK]),
                                  ALU.mult))
            rank = bank[0][:, 0:E * NT].rearrange("p (e t) -> p e t", e=E)
            eng.wait_ge(pe_rank, 1)
            own(eng.tensor_tensor_scan(inc[:, :, :].rearrange("p e t -> p (e t)"), c_seg, bank[1][:, 0:E * NT], 0.0,
                                       ALU.mult, ALU.add))
            own.done()
            own(eng.tensor_scalar(cnt[:, :], inc[:, :, NT - 1], float(P - 1), None, ALU.add))
            own.done()
            own(eng.tensor_copy(cnti[:, :], cnt[:, :]))
            own.done()
            own(eng.tensor_scalar(cnti[:, :], cnti[:, :], P - 1, None, ALU.bitwise_and))
            own.done()
            own(eng.tensor_copy(cmod[:, :], cnti[:, :]))
            own.done()
            own(eng.tensor_tensor(padded[:, :], cnt[:, :], cmod[:, :], ALU.subtract))
            own.done()
            one = kc[:, K_SEG + 1:K_SEG + 2].to_broadcast([P, E])
            own(eng.tensor_tensor_scan(pinc[:, :], one, padded[:, :], 0.0, ALU.mult, ALU.add))
            own(eng.tensor_tensor(pos[:, :, :], rank, inc[:, :, :], ALU.add))
            own.done()
            own(eng.tensor_tensor(pbase[:, :], pinc[:, :], padded[:, :], ALU.subtract))
            own.done()
            own(eng.tensor_tensor(pos[:, :, :], pos[:, :, :], pbase[:, :].unsqueeze(2).to_broadcast([P, E, NT]), ALU.add))
            own.done()
            for r in range(TOPK):
                own(eng.tensor_tensor(picked[:, r, :, :], eq[:, r, :, :], pos[:, :, :], ALU.mult))
            own.done()
            for r in range(TOPK):
                own(eng.reduce_sum(posf[:, r * NT:(r + 1) * NT], picked[:, r, :, :].rearrange("p e t -> p t e"), AX.X))
            own.done()
            own(eng.tensor_copy(slots[:, :, :].rearrange("p r t -> p (r t)"), posf[:, :]))
            own.done()
            own(eng.tensor_scalar(prowi[:, :], slots[:, :, :].rearrange("p r t -> p (r t)"), P - 1, None,
                                  ALU.bitwise_and))
            own.done()
            own(eng.tensor_copy(prow[:, :], prowi[:, :]))
            own.done()
            own(eng.tensor_tensor(pblk[:, :], posf[:, :], prow[:, :], ALU.subtract))
            own.done()
            for r in range(TOPK):
                ns = slice(r * NT, (r + 1) * NT)
                own(eng.tensor_tensor(ohr[:, ns, :], kr16[:, :].unsqueeze(1).to_broadcast([P, NT, P]),
                                      prow[:, ns].unsqueeze(2).to_broadcast([P, NT, P]), ALU.is_equal))
                own(eng.tensor_tensor(ohb[:, r, :, :], kb16[:, :].unsqueeze(1).to_broadcast([P, NT, NBLK]),
                                      pblk[:, ns].unsqueeze(2).to_broadcast([P, NT, NBLK]), ALU.is_equal))
                own.done()
                ins = eng.tensor_tensor(ohb[:, r, :, :], ohb[:, r, :, :],
                                        c_tok.unsqueeze(2).to_broadcast([P, NT, NBLK]), ALU.mult)
                ins.then_inc(dve_oh, 1)
            eng.wait_ge(pe_perm, 1)
            eng.tensor_copy(perm[:, :], bank[2][:, 0:NBLK]).then_inc(dve_perm, 1)
            own(eng.tensor_tensor(blk_eq[:, :, :], pinc[0:1, :].unsqueeze(1).to_broadcast([1, NBLK, E]),
                                  c_b[0:1, :].unsqueeze(2).to_broadcast([1, NBLK, E]), ALU.is_le))
            own.done()
            own(eng.reduce_sum(esum[:, :], blk_eq[:, :, :], AX.X))
            own.done()
            own(eng.tensor_scalar(esum[:, :], esum[:, :], float(E - 1), float(EXP_COLS), ALU.min, ALU.mult))
            own.done()
            eng.tensor_copy(eoff[:, 2:2 + NBLK], esum[:, :]).then_inc(dve_perm, 1)

            def low_x(i, b):
                eng.wait_ge(b_xh, i + 1)
                eng.tensor_tensor(bxl[:, b, :, :], bank[b][:, 0:DK * P].rearrange("p (k n) -> p k n", k=DK),
                                  bxh[:, b, :, :].bitcast(F32), ALU.subtract).then_inc(b_xl, 1)

            def product(i, b):
                eng.wait_ge(b_si, i + 1)
                eng.tensor_tensor(bh[:, b, :], bank[2 + b][:, H:2 * H], bsg[:, b, :], ALU.mult).then_inc(b_h, 1)

            def low_h(i, b):
                eng.wait_ge(b_hh, i + 1)
                eng.tensor_tensor(bhl[:, b, :], bank[4 + b][:, 0:P], bhh[:, b, :].bitcast(F32),
                                  ALU.subtract).then_inc(b_hl, 1)

            def check_panel(w, c, rounded):
                eng.wait_ge(act_pan, w + 1)
                eng.scalar_tensor_tensor(panel_stage(c), panel_stage(c), 1.0, rounded.bitcast(F32), ALU.mult,
                                         ALU.not_equal, accum_out=diff[:, bass.ds(w, 1)]).then_inc(dve_pan, 1)

            def dve_block(i, c):
                whole = isinstance(i, int)
                if not whole or i + 1 < NBLK:
                    low_x(i + 1, (c + 1) % 2)
                if not whole:
                    check_panel(i - 1, c - 1, Wr[:, bass.ds((i - 1) * PANEL, PANEL)])
                elif i - 1 in range(NPAN):
                    check_panel(i - 1, c - 1, panel_place(i - 1))
                if not whole or 0 <= i < NBLK:
                    product(i, c % 2)
                if not whole or 1 <= i <= NBLK:
                    low_h(i - 1, (c - 1) % 2)

            eng.wait_ge(dve_perm, 2)
            blocks(eng, dve_block, NBLK + 1)
            own(eng.reduce_max(flagf[:, 0:1], diff[:, :], AX.X))
            own.done()
            eng.tensor_scalar(flagf[:, 0:1], flagf[:, 0:1], 1.0, None, ALU.min).then_inc(dve_flag, 1)
            own.restart()

            def x2(g):
                def make(j):
                    eng.wait_ge(dma_yg[j], 16 * TOPK * g + 16 * TOPK)
                    for r, src in enumerate((xn, y2)):
                        if r:
                            own.done()
                        w = wtop[:, bass.ds(g * TG + j, 1), r:r + 1].rearrange("p a b -> p (a b)")
                        own(eng.scalar_tensor_tensor(tiles(g)(j), src[:, j, :], w, tiles(g)(j), ALU.mult, ALU.add))

                statistics(eng, own, tiles(g), 2, g, make)

            def low3(g):
                for k in range(DK):
                    eng.wait_ge(n_h3, DK * g + k + 1)
                    ins = eng.tensor_tensor(xTl[:, k, :], bank[6 + k][:, :], xTh[:, k, :].bitcast(F32), ALU.subtract)
                    if k < DK - 1:
                        own(ins)
                ins.then_inc(n_l3, 1)

            def x3(g):
                def make(j):
                    if j % 2 == 0:
                        eng.wait_ge(n_row, g + 1)
                        eng.wait_ge(n_p1, 2 * g + j // 2 + 1)
                        rows_ = X[:, bass.ds(g * TG + j, 2), :].rearrange("p a d -> p (a d)")
                        own(eng.scalar_tensor_tensor(rows_, bank[6 + j // 2][:, :], tg[:, 1:2], rows_, ALU.mult, ALU.add))

                statistics(eng, own, tiles(g), 3, g, make)

            def low4(g):
                for k in range(DK):
                    eng.wait_ge(n_h4, DK * g + k + 1)
                    ins = eng.tensor_tensor(xTl[:, k, :], bank[6 + k][:, :], xTh[:, k, :].bitcast(F32), ALU.subtract)
                    if k < DK - 1:
                        own(ins)
                ins.then_inc(n_l4, 1)

            def ffn(g, more):
                g3 = 3 * g
                for m in range(FK + 1):
                    if m < FK:
                        eng.wait_ge(f_act[m], g3 + 2)
                        eng.scalar_tensor_tensor(sg[:, m % 3, :], bank[2 * (m % 2) + 1][:, :], colv[:, C_S2 + m:C_S2 + m + 1],
                                                 sg[:, m % 3, :], ALU.mult, ALU.mult).then_inc(f_h[m], 1)
                    if m > 0:
                        eng.wait_ge(f_hh[m - 1], g + 1)
                        eng.tensor_tensor(hA[1][:, m - 1, :], sg[:, (m - 1) % 3, :], hA[0][:, m - 1, :].bitcast(F32),
                                          ALU.subtract).then_inc(f_hl[m - 1], 1)
                for layer, h in ((1, hB), (2, hA)):
                    for m in range(FK):
                        if layer == 1 and m == 0:
                            eng.wait_ge(f_dma, 16 * g + 16)
                        r = (8 * layer + m) % 3
                        eng.wait_ge(f_act[m], g3 + (layer + 2))
                        own(eng.tensor_copy(h[0][:, m, :], sg[:, r, :]))
                        own.done()
                        eng.tensor_tensor(h[1][:, m, :], sg[:, r, :], h[0][:, m, :].bitcast(F32),
                                          ALU.subtract).then_inc(f_hl[m], 1)
                        if more and layer == 1 and m == 1:
                            x2(g + 1)
                        if more and layer == 1 and m == 7:
                            low3(g + 1)
                        if more and layer == 2 and m == 2:
                            x3(g + 1)
                if more:
                    low4(g + 1)
                for q in range(2):
                    eng.wait_ge(f_w3[q], g + 1)
                    ins = eng.tensor_tensor(outb[:, 2 * q:2 * q + 2, :], bank[4 + q][:, :].rearrange("p (t d) -> p t d", t=2),
                                            w3s[:, :].unsqueeze(1).to_broadcast([P, 2, D]), ALU.mult)
                    ins.then_inc(f_w3r, 1)
                    if not more:
                        half = slice(2 * q, 2 * q + 2)
                        eng.wait_ge(f_w3r, 2 * g + q + 2)
                        eng.tensor_tensor(outb[:, half, :], outb[:, half, :], X[:, g * TG + 2 * q:g * TG + 2 * q + 2, :],
                                          ALU.add).then_inc(f_out, 1)
                own.restart()

            x2(0)
            low3(0)
            x3(0)
            low4(0)
            own.restart()
            with eng.Fori(0, NG - 1) as g:
                ffn(g, True)
            ffn(NG - 1, False)

        @block.scalar
        def _(eng):
            def norm(src, dst, which, g):
                normalise(eng, src, dst, which, g)

            done = [0]

            def split_high(n):
                for e in range(done[0], min(E, done[0] + n)):
                    eng.wait_ge(dma_exp[e % NES], 16 * (e // NES + 1))
                    eng.activation(EH[:, e * EXP_COLS:(e + 1) * EXP_COLS], ES[:, e % NES, :],
                                   ACT.Copy).then_inc(act_eh, 1)
                done[0] += n

            norm(tiles(0), lambda j: xa[:, 0, j, :], 0, 0)
            eng.wait_ge(pe_setup, 1)
            for d in range(DK):
                eng.activation(kT[:, d, :], bank[0][:, d * P:(d + 1) * P], ACT.Identity,
                               bias=colv[:, C_BK + d:C_BK + d + 1]).then_inc(act_setup, 1)
            def empty(dst, b, ready, n, done_sem):
                eng.wait_ge(ready, n)
                for k in range(DK):
                    ins = eng.activation(dst[:, k, :], bank[b + k][:, :], ACT.Copy)
                    ins.then_inc(done_sem, 1)

            for k in range(NG + 3):
                if k < NG:
                    empty(xaT, 0, pe_xaT, k + 1, act_xaT)
                if 1 <= k <= NG:
                    eng.wait_ge(pe_pT, k)
                    eng.activation(pT[:, :], bank[3][0:KEYS, :], ACT.Copy).then_inc(act_pT, 1)
                if 2 <= k < NG + 2:
                    norm(tiles(k - 2), lambda j: xb[:, k - 2, j, :], 1, k - 2)
                if k >= 3:
                    rows_ = lt[:, (k - 3) * TG:(k - 2) * TG, :]
                    eng.wait_ge(dve_lt, k - 2)
                    eng.activation(rows_, rows_, ACT.Exp).then_inc(act_lt, 1)
                split_high(1)
                if k + 1 < NG:
                    if k >= 1:
                        eng.wait_ge(pe_xaT, k)
                    norm(tiles(k + 1), lambda j: xa[:, (k + 1) % 2, j, :], 0, k + 1)
                if 2 <= k < NG + 2:
                    empty(xbT, 0, pe_xbT, k - 1, act_xbT)
                if k < NG:
                    eng.wait_ge(dve_s, k + 1)
                    eng.activation(pr[:, k % 2, :, :], pr[:, k % 2, :, :], ACT.Exp).then_inc(act_p, 1)
                if k == 0:
                    eng.wait_ge(pe_setup, 4)
                    eng.activation(tg[:, :], bank[6][:, D:D + 4], ACT.Tanh).then_inc(act_setup, 1)
                split_high({NG: 0, NG + 1: E}.get(k, 2))

            def high_x(i, b):
                eng.wait_ge(b_tx, i + 1)
                eng.activation(bxh[:, b, :, :].rearrange("p k n -> p (k n)"), bank[b][:, 0:DK * P],
                               ACT.Copy).then_inc(b_xh, 1)

            def silu(i, b):
                eng.wait_ge(b_gu, i + 1)
                eng.activation(bsg[:, b, :], bank[2 + b][:, 0:H], ACT.Silu).then_inc(b_si, 1)

            def high_h(i, b):
                eng.wait_ge(b_th, i + 1)
                eng.activation(bhh[:, b, :], bank[4 + b][:, 0:P], ACT.Copy).then_inc(b_hh, 1)

            def rows_out(i, b, c4):
                eng.wait_ge(b_y, i + 1)
                eng.wait_ge(dma_ys[c4 % 4], 16 * (i // 4) + 16 if isinstance(i, int) else 4 * (i - c4) + 16 * (c4 // 4) + 16)
                eng.activation(yb[:, c4 % 4, :], bank[6 + b][:, 0:D], ACT.Copy).then_inc(b_ye, 1)

            def round_panel(w, c):
                eng.wait_ge(dma_pan[c % STAGES], 16 * (w // STAGES) + 16 if isinstance(w, int)
                            else 4 * (w - c) + 16 * (c // STAGES) + 16)
                dst = panel_place(w) if isinstance(w, int) else Wr[:, bass.ds(w * PANEL, PANEL)]
                if isinstance(w, int) and w >= NPAN - LATE + 2:
                    eng.wait_ge(dve_pan, w - 1)
                hold(eng, w)
                eng.activation(dst, panel_stage(c), ACT.Copy).then_inc(act_pan, 1)

            def act_block(i, c):
                whole = isinstance(i, int)
                if not whole or i + 1 < NBLK:
                    high_x(i + 1, (c + 1) % 2)
                if not whole or i in range(NPAN):
                    round_panel(i, c)
                if not whole or 0 <= i < NBLK:
                    silu(i, c % 2)
                if not whole or 1 <= i <= NBLK:
                    high_h(i - 1, (c - 1) % 2)
                if not whole or 2 <= i <= NBLK + 1:
                    rows_out(i - 2, c % 2, c - 2)

            eng.activation(unused[:, :], ones[:, 0:1], ACT.Silu)
            blocks(eng, act_block, NBLK + 1)

            def norm3(g):
                norm(tiles(g), lambda j: xn[:, j, :], 2, g)

            def norm4(g):
                norm(tiles(g), lambda j: xn[:, j, :], 3, g)

            def high(g, ready, done_sem):
                eng.wait_ge(ready, g + 1)
                for k in range(DK):
                    eng.activation(xTh[:, k, :], bank[6 + k][:, :], ACT.Copy).then_inc(done_sem, 1)

            def ffn(g, more):
                g3 = 3 * g
                for m in range(FK + 1):
                    if m < FK:
                        eng.wait_ge(f_pe[m], g3 + 1)
                        if m < 3:
                            eng.wait_ge(f_hl[m + 5], g3 + 1)
                        else:
                            eng.wait_ge(f_hl[m - 3], g3 + 1 + 1)
                        eng.activation(sg[:, m % 3, :], bank[2 * (m % 2)][:, :], ACT.Silu,
                                       scale=colv[:, C_S1 + m:C_S1 + m + 1]).then_inc(f_act[m], 1)
                    if m > 0:
                        eng.wait_ge(f_h[m - 1], g + 1)
                        eng.activation(hA[0][:, m - 1, :], sg[:, (m - 1) % 3, :], ACT.Copy).then_inc(f_hh[m - 1], 1)
                for layer, c in ((1, C_H1), (2, C_H2)):
                    for m in range(FK):
                        eng.wait_ge(f_pe[m], g3 + (layer + 1))
                        if m < 3:
                            eng.wait_ge(f_hl[m + 5], g3 + layer + 1)
                        else:
                            eng.wait_ge(f_hl[m - 3], g3 + (layer + 1) + 1)
                        eng.activation(sg[:, (8 * layer + m) % 3, :], bank[m % 4][:, :], ACT.Gelu,
                                       scale=colv[:, c + m:c + m + 1]).then_inc(f_act[m], 1)
                        if more and layer == 1 and m == 3:
                            norm3(g + 1)
                        if more and layer == 1 and m == 7:
                            high(g + 1, n_T, n_h3)
                        if more and layer == 2 and m == 4:
                            norm4(g + 1)
                if more:
                    high(g + 1, n_T4, n_h4)

            norm3(0)
            high(0, n_T, n_h3)
            norm4(0)
            high(0, n_T4, n_h4)
            with eng.Fori(0, NG - 1) as g:
                ffn(g, True)
            ffn(NG - 1, False)

        @block.tensor
        def _(eng):
            mm = eng.matmul

            def three(dst, lhs, rhs, first, last):
                mm(dst, lhs[0], rhs[1], start=first, stop=False)
                mm(dst, lhs[1], rhs[0], start=False, stop=False)
                return mm(dst, lhs[0], rhs[0], start=False, stop=last)

            eng.wait_ge(dma_k, 16 * KEY_LOADS)
            eng.wait_ge(pool_const, 1)
            for d in range(DK):
                for k in range(DK):
                    ins = mm(bank[0][:, d * P:(d + 1) * P], WkT[:, k, d * P:(d + 1) * P], ctxTs[:, k, :],
                             start=k == 0, stop=k == DK - 1)
            ins.then_inc(pe_setup, 1)
            eng.wait_ge(act_setup, 2)
            for c in range(DK):
                for k in range(DK):
                    mm(bank[4][:, c * P:(c + 1) * P], Wq[:, k, c * P:(c + 1) * P], kT[:, k, :], start=k == 0, stop=k == DK - 1)
            for k in range(DK):
                ins = mm(bank[5][0:1, 0:P], colv[:, C_BQ + k:C_BQ + k + 1], kT[:, k, :], start=k == 0, stop=k == DK - 1)
            ins.then_inc(pe_setup, 1)

            def rest_of_setup():
                eng.wait_ge(dma_w, 16 * OTHER_LOADS)
                for b in range(NB):
                    dst = bank[7][0:KEYS, b * D:(b + 1) * D]
                    mm(dst, ones[:, 0:KEYS], rowv[:, R_BV:R_BV + D], start=True, stop=False)
                    for k in range(DK):
                        mm(dst, ctxTs[:, k, b * KEYS:(b + 1) * KEYS], WvT[:, k, :], start=False, stop=k == DK - 1)
                mm(bank[6][:, 0:D + 4], ones[:, :], rowv[:, R_S3:R_G + 4], start=True, stop=True).then_inc(pe_setup, 1)
                for b in range(NB):
                    dst = bank[3][:, b * D:(b + 1) * D]
                    mm(dst, ones[:, :], rowv[:, R_B1:R_B1 + D], start=True, stop=False)
                    for k in range(DK):
                        ins = mm(dst, cmean[:, k * NB + b, :], W2T[:, k, :], start=False, stop=k == DK - 1)
                ins.then_inc(pe_setup, 1)

            def transposes(src, b, which, g, sem_done):
                for j in range(TG):
                    eng.wait_ge(ln_done[which], TG * g + j + 1)
                    for k in range(DK):
                        ins = eng.transpose(bank[b + k][:, j * P:(j + 1) * P], src[:, j, k * P:(k + 1) * P], ident[:, :])
                ins.then_inc(sem_done, 1)

            def keep_clock(dst, n):
                for _ in range(n):
                    mm(dst[:, 0:P], ident[:, :], ident[:, :], start=True, stop=True)

            def scores(g):
                b = g // (NG // NB)
                eng.wait_ge(dve_s, g)
                keep_clock(bank[2], 4)
                eng.wait_ge(act_xaT, 2 * g + 2)
                mm(bank[2][:, 0:TG * KEYS], ones[:, :], qkrow[:, b, :, :].rearrange("p t n -> p (t n)"),
                   start=True, stop=False, skip_group_check=True)
                for j in range(TG):
                    for k in range(DK):
                        ins = mm(bank[2][:, j * KEYS:(j + 1) * KEYS], xaT[:, k, j * P:(j + 1) * P],
                                 QK[:, k, b * KEYS:(b + 1) * KEYS], start=False,
                                 stop=k == DK - 1, skip_group_check=True)
                ins.then_inc(pe_s, 1)

            def attend(g):
                b = g // (NG // NB)
                if g > 0:
                    eng.wait_ge(ln_var[1], g)
                keep_clock(bank[4], 4)
                eng.wait_ge(act_pT, g + 1)
                for j in range(TG):
                    ins = mm(bank[4 + j // 2][:, (j % 2) * D:(j % 2 + 1) * D], pT[:, j * P:(j + 1) * P], V[:, b, :],
                             start=True, stop=True)
                    if j % 2:
                        ins.then_inc(pe_o, 1)

            def logits(g):
                if g >= 2:
                    eng.wait_ge(dve_lt, g - 1)
                keep_clock(bank[6 + g % 2], 4)
                eng.wait_ge(act_xbT, 2 * g + 2)
                for j in range(TG):
                    for k in range(DK):
                        ins = mm(bank[6 + g % 2][:, j * E:(j + 1) * E], xbT[:, k, j * P:(j + 1) * P], gw[:, k, :],
                                 start=k == 0, stop=k == DK - 1)
                ins.then_inc(pe_lg, 1)

            for k in range(NG + 2):
                if k < NG:
                    if k >= 3:
                        eng.wait_ge(act_xbT, 2 * (k - 2))
                    transposes(xa[:, k % 2, :, :], 0, 0, k, pe_xaT)
                if k == 0:
                    eng.wait_ge(dve_setup, 2)
                if k == 1:
                    eng.wait_ge(dve_setup, 3)
                if 1 <= k <= NG:
                    eng.wait_ge(act_p, k)
                    for j in range(TG):
                        ins = eng.transpose(bank[3][0:KEYS, j * P:(j + 1) * P], pr[:, (k - 1) % 2, j, :], ident[:, :])
                    ins.then_inc(pe_pT, 1)
                if 1 <= k <= NG:
                    attend(k - 1)
                if k < NG:
                    scores(k)
                if k == 0:
                    rest_of_setup()
                if k >= 2:
                    if k >= NG:
                        eng.wait_ge(act_xbT, 2 * (k - 2))
                    transposes(xb[:, k - 2, :, :], 0, 1, k - 2, pe_xbT)
                    logits(k - 2)

            keep_clock(bank[0], 8)
            eng.wait_ge(dve_both, NG)
            rhs = both[:, :, :].rearrange("p e t -> p (e t)")
            mm(bank[0][:, 0:E * NT], kc[:, K_TRI:K_TRI + P], rhs, start=True, stop=True)
            mm(bank[1][:, 0:E * NT], ones128[:, :], rhs, start=True, stop=True).then_inc(pe_rank, 1)
            for n in range(TOPK * NT):
                if n % NT == 0:
                    eng.wait_ge(dve_oh, n // NT + 1)
                ins = mm(bank[2][:, 0:NBLK], ohr[:, n, :], ohb[:, n // NT, n % NT, :], start=n == 0, stop=n == TOPK * NT - 1)
            ins.then_inc(pe_perm, 1)

            def load_offsets(i, c):
                _, values = nc.values_load_multi_w_load_instructions(
                    eoff[0:1, bass.ds(i, BODY + 2)], engines=(mybir.EngineType.PE,), min_val=0, max_val=(E - 1) * EXP_COLS,
                    skip_runtime_bounds_check_because="DVE has bounded them")
                offsets.clear()
                offsets.update({c - 2 + n: v for n, v in enumerate(values)})

            def x_columns(i, b, c4):
                eng.wait_ge(dma_xg[c4 % 4], 16 * (i // 4) + 16 if isinstance(i, int) else 4 * (i - c4) + 16 * (c4 // 4) + 16)
                if not isinstance(i, int) or i >= 2:
                    eng.wait_ge(b_xl, i - 1)
                for k in range(DK):
                    ins = eng.transpose(bank[b][:, k * P:(k + 1) * P], xg[:, c4 % 4, k * P:(k + 1) * P], ident[:, :])
                ins.then_inc(b_tx, 1)

            def gate_up(i, b, at_):
                eng.wait_ge(b_xl, i + 1)
                if not isinstance(i, int) or i >= 2:
                    eng.wait_ge(b_h, i - 1)
                for k in range(DK):
                    w = bass.ds(at_ + k * 2 * H, 2 * H)
                    ins = three(bank[2 + b][:, 0:2 * H], (bxh[:, b, k, :], bxl[:, b, k, :]), (EH[:, w], EL[:, w]),
                                k == 0, k == DK - 1)
                ins.then_inc(b_gu, 1)

            def h_columns(i, b):
                eng.wait_ge(b_h, i + 1)
                if not isinstance(i, int) or i >= 2:
                    eng.wait_ge(b_hl, i - 1)
                eng.transpose(bank[4 + b][:, 0:P], bh[:, b, :], ident[:, :]).then_inc(b_th, 1)

            def down(i, b, at_):
                eng.wait_ge(b_hl, i + 1)
                if not isinstance(i, int) or i >= 2:
                    eng.wait_ge(b_ye, i - 1)
                w = bass.ds(at_ + 2 * DK * H, D)
                three(bank[6 + b][:, 0:D], (bhh[:, b, :], bhl[:, b, :]), (EH[:, w], EL[:, w]), True, True).then_inc(b_y, 1)

            def pe_block(i, c):
                whole = isinstance(i, int)
                if not whole or i + 1 < NBLK:
                    x_columns(i + 1, (c + 1) % 2, c + 1)
                if not whole or 0 <= i < NBLK:
                    gate_up(i, c % 2, offsets[c])
                if not whole or 1 <= i <= NBLK:
                    h_columns(i - 1, (c - 1) % 2)
                if not whole or 2 <= i <= NBLK + 1:
                    down(i - 2, c % 2, offsets[c - 2])

            offsets = {}
            eng.wait_ge(dve_perm, 2)
            eng.wait_ge(pool_el, E)
            blocks(eng, pe_block, NBLK + 1, load_offsets)

            def T3(g):
                if not (isinstance(g, int) and g == 0):
                    eng.wait_ge(n_l4, g)
                transposes(xn, 6, 2, g, n_T)

            def part1(g):
                eng.wait_ge(n_l3, g + 1)
                for j in range(TG):
                    dst = bank[6 + j // 2][:, (j % 2) * D:(j % 2 + 1) * D]
                    for k in range(DK):
                        ins = three(dst, (xTh[:, k, j * P:(j + 1) * P], xTl[:, k, j * P:(j + 1) * P]),
                                    (W1h[:, k, :], W1l[:, k, :]), k == 0, k == DK - 1)
                    if j % 2:
                        ins.then_inc(n_p1, 1)

            def T4(g):
                transposes(xn, 6, 3, g, n_T4)

            def ffn(g, more, general):
                g3 = 3 * g
                panel = [0]

                def low_part():
                    w = panel[0]
                    panel[0] += 1
                    eng.wait_ge(lo_ready, g * NPAN + (w + 3))
                    return Wlo[:, w % 2, :]

                for m in range(FK):
                    if m >= 2:
                        eng.wait_ge(f_h[m - 2], g + 1)
                    elif m == 0:
                        eng.wait_ge(n_l4, g + 1)
                        eng.wait_ge(f_act[5], g3 + 1)
                    else:
                        eng.wait_ge(f_act[7], g3 + 1)
                    w = Wr[:, m * PANEL:(m + 1) * PANEL].rearrange("p (u k n) -> p u k n", u=2, k=DK)
                    lo = low_part().rearrange("p (u k n) -> p u k n", u=2, k=DK) if general else None
                    for u in range(2):
                        dst = bank[2 * (m % 2) + u][:, :]
                        for k in range(DK):
                            mm(dst, w[:, u, k, :], xTh[:, k, :], start=k == 0, stop=False)
                            ins = mm(dst, w[:, u, k, :], xTl[:, k, :], start=False, stop=k == DK - 1 and not general)
                            if general:
                                ins = mm(dst, lo[:, u, k, :], xTh[:, k, :], start=False, stop=k == DK - 1)
                    ins.then_inc(f_pe[m], 1)
                    if general:
                        eng.wait_ge(f_pe[m], g3 + 1)
                        eng.sem_inc(lo_used, 1)
                for layer, h in ((1, hA), (2, hB)):
                    if layer == 2:
                        eng.wait_ge(pool_late, LATE)
                    for m in range(FK):
                        if m < 4:
                            if layer == 1:
                                eng.wait_ge(f_h[6 + m // 2], g + 1)
                            else:
                                eng.wait_ge(f_act[m + 4], g3 + 2 + 1)
                        else:
                            eng.wait_ge(f_act[m - 4], g3 + (layer + 1) + 1)
                        for q in range(2):
                            lo = low_part().rearrange("p (k n) -> p k n", k=4) if general else None
                            for kk in range(4):
                                k = 4 * q + kk
                                base = ((2 * layer - 1) * FK + 2 * m + q) * PANEL + kk * P
                                if m == 0:
                                    eng.wait_ge(f_hl[k], g3 + layer + 1)
                                mm(bank[m % 4][:, :], Wr[:, base:base + P], h[0][:, k, :], start=k == 0, stop=False)
                                ins = mm(bank[m % 4][:, :], Wr[:, base:base + P], h[1][:, k, :], start=False,
                                         stop=k == FK - 1 and not general)
                                if general:
                                    ins = mm(bank[m % 4][:, :], lo[:, kk, :], h[0][:, k, :], start=False, stop=k == FK - 1)
                            if general and q == 0:
                                ins.then_inc(lo_used, 1)
                        ins.then_inc(f_pe[m], 1)
                        if general:
                            eng.wait_ge(f_pe[m], g3 + (layer + 1))
                            eng.sem_inc(lo_used, 1)
                        if more and layer == 1 and m == 6:
                            T3(g + 1)
                        if more and layer == 2 and m == 1:
                            part1(g + 1)
                        if more and layer == 2 and m == 6:
                            T4(g + 1)
                eng.wait_ge(f_w3r, 2 * g + 1)
                base = 5 * FK * PANEL
                if not general:
                    for j, chunks in ((0, range(FK - 1)), (2, range(FK - 1)), (0, [FK - 1]), (1, range(FK)),
                                      (2, [FK - 1]), (3, range(FK))):
                        for k in chunks:
                            if j == 0:
                                eng.wait_ge(f_hl[k], g3 + 3 + 1)
                            w = Wr[:, base + k * D:base + (k + 1) * D]
                            dst = bank[4 + j // 2][:, (j % 2) * D:(j % 2 + 1) * D]
                            mm(dst, hA[0][:, k, j * P:(j + 1) * P], w, start=k == 0, stop=False)
                            ins = mm(dst, hA[1][:, k, j * P:(j + 1) * P], w, start=False, stop=k == FK - 1)
                        if j % 2:
                            ins.then_inc(f_w3[j // 2], 1)
                else:
                    for k in range(FK):
                        if k % 2 == 0:
                            lo = low_part().rearrange("p (k n) -> p k n", k=2)
                        eng.wait_ge(f_hl[k], g3 + 3 + 1)
                        w = Wr[:, base + k * D:base + (k + 1) * D]
                        for j in range(TG):
                            dst = bank[4 + j // 2][:, (j % 2) * D:(j % 2 + 1) * D]
                            mm(dst, hA[0][:, k, j * P:(j + 1) * P], w, start=k == 0 and j % 2 == 0, stop=False,
                               skip_group_check=True)
                            mm(dst, hA[1][:, k, j * P:(j + 1) * P], w, start=False, stop=False, skip_group_check=True)
                            ins = mm(dst, hA[0][:, k, j * P:(j + 1) * P], lo[:, k % 2, :], start=False, stop=k == FK - 1,
                                     skip_group_check=True)
                            if k == FK - 1 and j % 2:
                                ins.then_inc(f_w3[j // 2], 1)
                        if k % 2 and k < FK - 1:
                            ins.then_inc(lo_used, 1)
                    eng.wait_ge(f_w3[1], g + 1)
                    eng.sem_inc(lo_used, 1)

            eng.wait_ge(b_ye, NBLK)
            eng.wait_ge(ln_var[2], 1)
            keep_clock(bank[6], 7)
            T3(0)
            keep_clock(bank[0], 8)
            part1(0)
            keep_clock(bank[0], 20)
            T4(0)
            keep_clock(bank[0], 10)
            eng.wait_ge(act_pan, NPAN)
            eng.wait_ge(pool_flag, 1)
            general_flag = eng.value_load(flag[0:1, 0:1], min_val=0, max_val=1)
            with eng.If(general_flag == 1):
                with eng.Fori(0, NG - 1) as g:
                    ffn(g, True, True)
                ffn(NG - 1, False, True)
            with eng.Else():
                with eng.Fori(0, NG - 1) as g:
                    ffn(g, True, False)
                ffn(NG - 1, False, False)


def kernel(**inputs):
    import numpy as np
    import concourse.bacc as bacc
    from concourse import mybir as mb
    from concourse.bass_utils import run_bass_kernel_spmd

    v = {k: np.asarray(a) for k, a in inputs.items()}
    con = np.ascontiguousarray

    def vec(a):
        return con(a.reshape(-1, P).T)

    def row(a):
        return a.reshape(1, -1)

    experts = np.concatenate([
        np.stack([v["L0_ffn_w1"].reshape(E, DK, P, H), v["L0_ffn_w3"].reshape(E, DK, P, H)], 3)
        .transpose(0, 2, 1, 3, 4).reshape(E, P, DK * 2 * H), v["L0_ffn_w2"]], 2)

    def kxm(w):
        return w.T.reshape(w.shape[1] // P, P, w.shape[0] // P, P)

    w12 = np.stack([kxm(v["L1_ffn_w1_w"]), kxm(v["L1_ffn_w2_w"])], 0)
    w12 = w12.transpose(3, 2, 0, 1, 4).reshape(FK, P, PANEL)
    hs = [kxm(v[n]).transpose(2, 1, 0, 3).reshape(FK, P, 2, PANEL).transpose(0, 2, 1, 3).reshape(2 * FK, P, PANEL)
          for n in ("L1_ffn_h1_w", "L1_ffn_h2_w")]
    w3 = v["L1_ffn_w3_w"].T.reshape(FK // 2, 2, P, D).transpose(0, 2, 1, 3).reshape(FK // 2, P, PANEL)
    arrays = {
        "x": v["x"].reshape(T, D),
        "ctxT": v["ctx_1024"].reshape(NB * KEYS, D).T,
        "cols": np.concatenate([vec(v[n]) for n in ("L0_xattn_bq", "L0_xattn_bk", "L1_ffn_w1_s", "L1_ffn_w2_s",
                                                    "L1_ffn_h1_s", "L1_ffn_h2_s")], 1),
        "rows": np.concatenate([row(v[n]) for n in ("L0_xattn_bv", "L1_xattn_b", "L1_ffn_w3_s", "g_xattn", "g_ffn")], 1),
        "wq": v["L0_xattn_Wq"],
        "wkT": v["L0_xattn_Wk"].T,
        "wvT": v["L0_xattn_Wv"].T,
        "gate": v["L0_ffn_gate_w"],
        "experts": experts,
        "w1T": v["L1_xattn_W"][:, :D].T,
        "w2T": v["L1_xattn_W"][:, D:].T,
        "panels": np.concatenate([w12, *hs, w3], 0),
    }
    r, seg = np.arange(P), np.arange(E * NT) % NT != 0
    arrays["consts"] = np.concatenate([
        (r[:, None] < r[None, :]) - 1, np.tile(r, (P, 1)), np.tile(np.arange(NBLK) * P, (P, 1)), np.tile(np.arange(E), (P, 1)),
        np.arange(NT)[None, :] * P + r[:, None], np.tile(seg, (P, 1))], 1).astype(np.float32)
    arrays["identity"] = np.eye(P, dtype=np.float32)
    arrays = {k: con(a) for k, a in arrays.items()}
    nc = bacc.Bacc("TRN2", target_bir_lowering=False, num_devices=1)
    args = [nc.dram_tensor(k, a.shape, mb.dt.from_np(a.dtype), kind="ExternalInput").ap() for k, a in arrays.items()]
    out = nc.dram_tensor("out", (T, D), F32, kind="ExternalOutput").ap()
    flamingo_kernel(nc, *args, out)
    got = run_bass_kernel_spmd(nc, [arrays], core_ids=[0])
    return got.results[0]["out"].reshape(v["x"].shape)
```
